# Optimizing a Trainium2 kernel written in Bass

```python
import numpy as np
import jax
import jax.numpy as jnp

def _softmax(x, axis=-1):
    return jax.nn.softmax(x, axis=axis)

def _gelu(x):
    return jax.nn.gelu(x, approximate=True)

def _silu(x):
    return jax.nn.silu(x)

def _sigmoid(x):
    return jax.nn.sigmoid(x)

def _layernorm(x, axis=-1, eps=1e-05):
    m = jnp.mean(x, axis=axis, keepdims=True)
    v = jnp.var(x, axis=axis, keepdims=True)
    return (x - m) / jnp.sqrt(v + eps)

def _scatter_add(tgt, idx, src, axis=0):
    return tgt.at[idx].add(src)

def _segment_sum(src, seg, n):
    return jax.ops.segment_sum(src, seg, n)
kernel_name = 'mk_dlrm_tower_d1_rec_r8_5430c8'

def setup_inputs(seed: int=0):
    np.random.seed(seed)
    _w = jnp.asarray

    def _rec_inputs():
        import jax
        import jax.numpy as jnp
        _tk = jax.random.key(seed)
        dense_ctx = jax.random.normal(jax.random.fold_in(_tk, 190), (512, 16), jnp.float32)
        ids = jnp.stack([jax.random.randint(jax.random.fold_in(_tk, 200 + f), (512,), 0, v, jnp.int32) for f, v in enumerate([1250, 1250, 1000, 12500, 125000, 1250, 1000, 12500, 12500, 125000, 125000, 125000, 12500, 125000, 1250, 1250, 1000, 125000, 1000, 1250, 12500, 125000, 1000, 125000, 1000, 12500, 1000, 1000, 12500, 1250, 1250, 125000, 1000, 1000, 1250, 1250, 1000, 1250, 1250])], axis=1)
        tbl_0 = 0.05 * jax.random.normal(jax.random.fold_in(_tk, 500 + 0), (1250, 16), jnp.float32)
        tbl_1 = 0.05 * jax.random.normal(jax.random.fold_in(_tk, 500 + 1), (1250, 16), jnp.float32)
        tbl_2 = 0.05 * jax.random.normal(jax.random.fold_in(_tk, 500 + 2), (1000, 16), jnp.float32)
        tbl_3 = 0.05 * jax.random.normal(jax.random.fold_in(_tk, 500 + 3), (12500, 16), jnp.float32)
        tbl_4 = 0.05 * jax.random.normal(jax.random.fold_in(_tk, 500 + 4), (125000, 16), jnp.float32)
        tbl_5 = 0.05 * jax.random.normal(jax.random.fold_in(_tk, 500 + 5), (1250, 16), jnp.float32)
        tbl_6 = 0.05 * jax.random.normal(jax.random.fold_in(_tk, 500 + 6), (1000, 16), jnp.float32)
        tbl_7 = 0.05 * jax.random.normal(jax.random.fold_in(_tk, 500 + 7), (12500, 16), jnp.float32)
        tbl_8 = 0.05 * jax.random.normal(jax.random.fold_in(_tk, 500 + 8), (12500, 16), jnp.float32)
        tbl_9 = 0.05 * jax.random.normal(jax.random.fold_in(_tk, 500 + 9), (125000, 16), jnp.float32)
        tbl_10 = 0.05 * jax.random.normal(jax.random.fold_in(_tk, 500 + 10), (125000, 16), jnp.float32)
        tbl_11 = 0.05 * jax.random.normal(jax.random.fold_in(_tk, 500 + 11), (125000, 16), jnp.float32)
        tbl_12 = 0.05 * jax.random.normal(jax.random.fold_in(_tk, 500 + 12), (12500, 16), jnp.float32)
        tbl_13 = 0.05 * jax.random.normal(jax.random.fold_in(_tk, 500 + 13), (125000, 16), jnp.float32)
        tbl_14 = 0.05 * jax.random.normal(jax.random.fold_in(_tk, 500 + 14), (1250, 16), jnp.float32)
        tbl_15 = 0.05 * jax.random.normal(jax.random.fold_in(_tk, 500 + 15), (1250, 16), jnp.float32)
        tbl_16 = 0.05 * jax.random.normal(jax.random.fold_in(_tk, 500 + 16), (1000, 16), jnp.float32)
        tbl_17 = 0.05 * jax.random.normal(jax.random.fold_in(_tk, 500 + 17), (125000, 16), jnp.float32)
        tbl_18 = 0.05 * jax.random.normal(jax.random.fold_in(_tk, 500 + 18), (1000, 16), jnp.float32)
        tbl_19 = 0.05 * jax.random.normal(jax.random.fold_in(_tk, 500 + 19), (1250, 16), jnp.float32)
        tbl_20 = 0.05 * jax.random.normal(jax.random.fold_in(_tk, 500 + 20), (12500, 16), jnp.float32)
        tbl_21 = 0.05 * jax.random.normal(jax.random.fold_in(_tk, 500 + 21), (125000, 16), jnp.float32)
        tbl_22 = 0.05 * jax.random.normal(jax.random.fold_in(_tk, 500 + 22), (1000, 16), jnp.float32)
        tbl_23 = 0.05 * jax.random.normal(jax.random.fold_in(_tk, 500 + 23), (125000, 16), jnp.float32)
        tbl_24 = 0.05 * jax.random.normal(jax.random.fold_in(_tk, 500 + 24), (1000, 16), jnp.float32)
        tbl_25 = 0.05 * jax.random.normal(jax.random.fold_in(_tk, 500 + 25), (12500, 16), jnp.float32)
        tbl_26 = 0.05 * jax.random.normal(jax.random.fold_in(_tk, 500 + 26), (1000, 16), jnp.float32)
        tbl_27 = 0.05 * jax.random.normal(jax.random.fold_in(_tk, 500 + 27), (1000, 16), jnp.float32)
        tbl_28 = 0.05 * jax.random.normal(jax.random.fold_in(_tk, 500 + 28), (12500, 16), jnp.float32)
        tbl_29 = 0.05 * jax.random.normal(jax.random.fold_in(_tk, 500 + 29), (1250, 16), jnp.float32)
        tbl_30 = 0.05 * jax.random.normal(jax.random.fold_in(_tk, 500 + 30), (1250, 16), jnp.float32)
        tbl_31 = 0.05 * jax.random.normal(jax.random.fold_in(_tk, 500 + 31), (125000, 16), jnp.float32)
        tbl_32 = 0.05 * jax.random.normal(jax.random.fold_in(_tk, 500 + 32), (1000, 16), jnp.float32)
        tbl_33 = 0.05 * jax.random.normal(jax.random.fold_in(_tk, 500 + 33), (1000, 16), jnp.float32)
        tbl_34 = 0.05 * jax.random.normal(jax.random.fold_in(_tk, 500 + 34), (1250, 16), jnp.float32)
        tbl_35 = 0.05 * jax.random.normal(jax.random.fold_in(_tk, 500 + 35), (1250, 16), jnp.float32)
        tbl_36 = 0.05 * jax.random.normal(jax.random.fold_in(_tk, 500 + 36), (1000, 16), jnp.float32)
        tbl_37 = 0.05 * jax.random.normal(jax.random.fold_in(_tk, 500 + 37), (1250, 16), jnp.float32)
        tbl_38 = 0.05 * jax.random.normal(jax.random.fold_in(_tk, 500 + 38), (1250, 16), jnp.float32)
        _rk = jax.random.fold_in(_tk, 7)
        W_top1 = 0.05 * jax.random.normal(jax.random.fold_in(_tk, 801), (400, 512), jnp.float32)
        W_top2 = 0.0441942 * jax.random.normal(jax.random.fold_in(_tk, 802), (512, 256), jnp.float32)
        W_top3 = 0.0625 * jax.random.normal(jax.random.fold_in(_tk, 803), (256, 1), jnp.float32)
        b_top1 = jnp.zeros((512,), jnp.float32)
        b_top2 = jnp.zeros((256,), jnp.float32)
        return (dense_ctx, ids, tbl_0, tbl_1, tbl_2, tbl_3, tbl_4, tbl_5, tbl_6, tbl_7, tbl_8, tbl_9, tbl_10, tbl_11, tbl_12, tbl_13, tbl_14, tbl_15, tbl_16, tbl_17, tbl_18, tbl_19, tbl_20, tbl_21, tbl_22, tbl_23, tbl_24, tbl_25, tbl_26, tbl_27, tbl_28, tbl_29, tbl_30, tbl_31, tbl_32, tbl_33, tbl_34, tbl_35, tbl_36, tbl_37, tbl_38, W_top1, b_top1, W_top2, b_top2, W_top3)
    dense_ctx, ids, tbl_0, tbl_1, tbl_2, tbl_3, tbl_4, tbl_5, tbl_6, tbl_7, tbl_8, tbl_9, tbl_10, tbl_11, tbl_12, tbl_13, tbl_14, tbl_15, tbl_16, tbl_17, tbl_18, tbl_19, tbl_20, tbl_21, tbl_22, tbl_23, tbl_24, tbl_25, tbl_26, tbl_27, tbl_28, tbl_29, tbl_30, tbl_31, tbl_32, tbl_33, tbl_34, tbl_35, tbl_36, tbl_37, tbl_38, W_top1, b_top1, W_top2, b_top2, W_top3 = _rec_inputs()

    def _L0_rec_setup():
        import jax, jax.numpy as jnp
        import numpy as np
        B, F0, D = (512, 39, 16)
        CIN = [128, 128, 128]

        def _cin_layer(X0, Xi, W, b):
            H = W.shape[0]
            F0_, Fi = (X0.shape[1], Xi.shape[1])
            Wr = W.reshape(H, F0_, Fi)
            return jnp.einsum('hjk,bjd,bkd->bhd', Wr, X0, Xi) + b[None, :, None]
        key = jax.random.key(seed)
        ks = jax.random.split(key, 4)
        x = jax.random.normal(ks[0], (B, F0, D), dtype=jnp.float32)
        fields = [F0] + CIN
        inp = {'embedded_features': x}
        for i in range(len(CIN)):
            cin = F0 * fields[i]
            cout = fields[i + 1]
            kw = jax.random.fold_in(ks[1], i)
            inp[f'W{i}'] = jax.random.normal(kw, (cout, cin), dtype=jnp.float32) / np.sqrt(cin)
            inp[f'b{i}'] = jnp.zeros((cout,), dtype=jnp.float32)
        return inp
    _L0_rec_all = _L0_rec_setup()
    _L0_rec_in = {k: v for k, v in _L0_rec_all.items() if k in ('W0', 'b0', 'W1', 'b1', 'W2', 'b2')}
    del _L0_rec_all
    return {'dense_ctx': dense_ctx, 'ids': ids, 'tbl_0': tbl_0, 'tbl_1': tbl_1, 'tbl_2': tbl_2, 'tbl_3': tbl_3, 'tbl_4': tbl_4, 'tbl_5': tbl_5, 'tbl_6': tbl_6, 'tbl_7': tbl_7, 'tbl_8': tbl_8, 'tbl_9': tbl_9, 'tbl_10': tbl_10, 'tbl_11': tbl_11, 'tbl_12': tbl_12, 'tbl_13': tbl_13, 'tbl_14': tbl_14, 'tbl_15': tbl_15, 'tbl_16': tbl_16, 'tbl_17': tbl_17, 'tbl_18': tbl_18, 'tbl_19': tbl_19, 'tbl_20': tbl_20, 'tbl_21': tbl_21, 'tbl_22': tbl_22, 'tbl_23': tbl_23, 'tbl_24': tbl_24, 'tbl_25': tbl_25, 'tbl_26': tbl_26, 'tbl_27': tbl_27, 'tbl_28': tbl_28, 'tbl_29': tbl_29, 'tbl_30': tbl_30, 'tbl_31': tbl_31, 'tbl_32': tbl_32, 'tbl_33': tbl_33, 'tbl_34': tbl_34, 'tbl_35': tbl_35, 'tbl_36': tbl_36, 'tbl_37': tbl_37, 'tbl_38': tbl_38, 'W_top1': W_top1, 'b_top1': b_top1, 'W_top2': W_top2, 'b_top2': b_top2, 'W_top3': W_top3, 'L0_rec_W0': _L0_rec_in['W0'], 'L0_rec_b0': _L0_rec_in['b0'], 'L0_rec_W1': _L0_rec_in['W1'], 'L0_rec_b1': _L0_rec_in['b1'], 'L0_rec_W2': _L0_rec_in['W2'], 'L0_rec_b2': _L0_rec_in['b2']}

def reference(dense_ctx, ids, tbl_0, tbl_1, tbl_2, tbl_3, tbl_4, tbl_5, tbl_6, tbl_7, tbl_8, tbl_9, tbl_10, tbl_11, tbl_12, tbl_13, tbl_14, tbl_15, tbl_16, tbl_17, tbl_18, tbl_19, tbl_20, tbl_21, tbl_22, tbl_23, tbl_24, tbl_25, tbl_26, tbl_27, tbl_28, tbl_29, tbl_30, tbl_31, tbl_32, tbl_33, tbl_34, tbl_35, tbl_36, tbl_37, tbl_38, W_top1, b_top1, W_top2, b_top2, W_top3, L0_rec_W0, L0_rec_b0, L0_rec_W1, L0_rec_b1, L0_rec_W2, L0_rec_b2):
    import jax
    import jax.numpy as jnp

    def _L0_rec_ref(embedded_features, W0, b0, W1, b1, W2, b2):
        import jax, jax.numpy as jnp
        import numpy as np
        B, F0, D = (512, 39, 16)
        CIN = [128, 128, 128]

        def _cin_layer(X0, Xi, W, b):
            H = W.shape[0]
            F0_, Fi = (X0.shape[1], Xi.shape[1])
            Wr = W.reshape(H, F0_, Fi)
            return jnp.einsum('hjk,bjd,bkd->bhd', Wr, X0, Xi) + b[None, :, None]
        X0 = embedded_features
        Ws = [(W0, b0), (W1, b1), (W2, b2)]
        Xi = X0
        res = []
        for W, b in Ws:
            Xi = _cin_layer(X0, Xi, W, b)
            res.append(Xi.sum(axis=2))
        return jnp.concatenate(res, axis=1)
    e = jnp.stack([tbl_0[ids[:, 0]], tbl_1[ids[:, 1]], tbl_2[ids[:, 2]], tbl_3[ids[:, 3]], tbl_4[ids[:, 4]], tbl_5[ids[:, 5]], tbl_6[ids[:, 6]], tbl_7[ids[:, 7]], tbl_8[ids[:, 8]], tbl_9[ids[:, 9]], tbl_10[ids[:, 10]], tbl_11[ids[:, 11]], tbl_12[ids[:, 12]], tbl_13[ids[:, 13]], tbl_14[ids[:, 14]], tbl_15[ids[:, 15]], tbl_16[ids[:, 16]], tbl_17[ids[:, 17]], tbl_18[ids[:, 18]], tbl_19[ids[:, 19]], tbl_20[ids[:, 20]], tbl_21[ids[:, 21]], tbl_22[ids[:, 22]], tbl_23[ids[:, 23]], tbl_24[ids[:, 24]], tbl_25[ids[:, 25]], tbl_26[ids[:, 26]], tbl_27[ids[:, 27]], tbl_28[ids[:, 28]], tbl_29[ids[:, 29]], tbl_30[ids[:, 30]], tbl_31[ids[:, 31]], tbl_32[ids[:, 32]], tbl_33[ids[:, 33]], tbl_34[ids[:, 34]], tbl_35[ids[:, 35]], tbl_36[ids[:, 36]], tbl_37[ids[:, 37]], tbl_38[ids[:, 38]]], axis=1)
    z = _L0_rec_ref(e, L0_rec_W0, L0_rec_b0, L0_rec_W1, L0_rec_b1, L0_rec_W2, L0_rec_b2)
    z = z.reshape(z.shape[0], -1)
    h = jnp.concatenate([z, dense_ctx], axis=1)
    h = jnp.maximum(h @ W_top1 + b_top1, 0.0)
    h = jnp.maximum(h @ W_top2 + b_top2, 0.0)
    y = h @ W_top3
    return y

_drawn_inputs = setup_inputs


def setup_inputs(seed=0):
    import zlib

    import numpy as np

    out = dict(_drawn_inputs(seed))
    spreads = {'b_top1': (0.0, 0.1),
     'b_top2': (0.0, 0.1),
     'L0_rec_b0': (0.0, 0.1),
     'L0_rec_b1': (0.0, 0.1),
     'L0_rec_b2': (0.0, 0.1)}
    factors = {'tbl_0': 8.0,
     'tbl_1': 5.92,
     'tbl_2': 5.193,
     'tbl_3': 7.212,
     'tbl_4': 8.0,
     'tbl_5': 8.0,
     'tbl_6': 8.0,
     'tbl_7': 6.869,
     'tbl_8': 8.0,
     'tbl_9': 8.0,
     'tbl_10': 8.0,
     'tbl_11': 6.68,
     'tbl_12': 8.0,
     'tbl_13': 8.0,
     'tbl_14': 4.334,
     'tbl_15': 5.734,
     'tbl_16': 8.0,
     'tbl_17': 8.0,
     'tbl_18': 8.0,
     'tbl_19': 6.14,
     'tbl_20': 7.189,
     'tbl_21': 8.0,
     'tbl_22': 8.0,
     'tbl_23': 8.0,
     'tbl_24': 8.0,
     'tbl_25': 7.106,
     'tbl_26': 5.656,
     'tbl_27': 8.0,
     'tbl_28': 8.0,
     'tbl_29': 8.0,
     'tbl_30': 6.865,
     'tbl_31': 6.307,
     'tbl_32': 8.0,
     'tbl_33': 6.282,
     'tbl_34': 8.0,
     'tbl_35': 7.605,
     'tbl_36': 8.0,
     'tbl_37': 6.41,
     'tbl_38': 8.0,
     'L0_rec_W0': 3.349,
     'L0_rec_W1': 2.695}
    for name, (base, spread) in spreads.items():
        noise = np.random.default_rng([zlib.crc32(name.encode()), seed]).standard_normal(out[name].shape)
        drawn = base * np.exp(spread * noise) if base else spread * noise
        out[name] = jnp.asarray(drawn.astype(out[name].dtype))
    for name, factor in factors.items():
        out[name] = (out[name] * factor).astype(out[name].dtype)
    return out
```

```python
import concourse.bass as bass
from concourse import mybir
from contextlib import ExitStack
import numpy as np

F32 = mybir.dt.float32
F32R = mybir.dt.float32r
I32 = mybir.dt.int32
ALU = mybir.AluOpType
ACT = mybir.ActivationFunctionType
AX = mybir.AxisListType

VOCAB = [1250, 1250, 1000, 12500, 125000, 1250, 1000, 12500, 12500, 125000, 125000, 125000, 12500,
         125000, 1250, 1250, 1000, 125000, 1000, 1250, 12500, 125000, 1000, 125000, 1000, 12500, 1000,
         1000, 12500, 1250, 1250, 125000, 1000, 1000, 1250, 1250, 1000, 1250, 1250]
B, NF, D, H = 512, 39, 16, 128
CTX = 16
T1, T2 = 512, 256
P = 128

TB = P // D
TG = 4
GB = TB * TG
NG = B // GB
NJ = 40
QF = NJ // 4
NCH = 7
FBLOCKS = [(0, 7), (7, 7), (14, 7), (21, 6), (27, 6), (33, 6)]
NPAIR = sum(m * (NF - a) for a, m in FBLOCKS)
assert (NCH - 1) * P < NPAIR <= NCH * P
NBK = 10
NS = TG * NBK
YB = 4

KIND = "VGDGDVGDVD"
FIELDS4 = [0, 1, 2, 9, 3, 4, 5, 6, 7, 8]
LAST4 = FIELDS4.index(9)
V_SLOTS = [k for k in range(NBK) if KIND[k] == "V"]
G_SLOTS = [k for k in range(NBK) if KIND[k] == "G"]
assert len(V_SLOTS) == 3 and G_SLOTS[1] == LAST4 and V_SLOTS[0] == 0 and KIND[2] == "D"
N_ACT = len(V_SLOTS) + len(G_SLOTS)
CHAIN_AFTER, n = {}, 0
for k in range(NBK):
    n += {"D": 4, "V": 1 if k else 0, "G": 0}[KIND[k]]
    CHAIN_AFTER[k] = n
CHAIN = n + 3
FOLD_IN = n

EXTRA = {0: [("T", 0)], 1: [("E", 0)], 2: [("E", 1)], 3: [("E", 2), ("M", 0)], 4: [("E", 3)],
         5: [("T", 1)], 6: [("E", 4)], 8: [("M", 1)], 10: [("T", 2)], 13: [("M", 2)], 15: [("T", 3)],
         18: [("M", 3)], 20: [("T", 4)], 23: [("M", 4)], 25: [("T", 5)], 28: [("M", 5)],
         29: [("T", 6)], 32: [("M", 6)]}
X1_SLOT = 33
G_SLOT = 4
UNITS = [e for s in range(NS) for e in EXTRA.get(s, []) if e[0] in "TE"]
NU = len(UNITS)
PRO_UNITS = [("E", k) for k in range(5)] * 2 + [("T", c) for c in range(NCH)]
NPU = len(PRO_UNITS)
NIDX = NG + 2


def count(g, per_group, within):
    return g * per_group + within


def build(nc, table, ids, first_row, ident_in, bmask_in, w0a, w0b, w1, w2, b0, b1, b2,
          wt1, wt1c, bt1, wt2, bt2, wt3, ctx_t, out):
    es = ExitStack()
    with es:
        def sb(name, shape, dt=F32):
            return es.enter_context(nc.sbuf_tensor(name, shape, dt))

        def pb(name):
            return es.enter_context(nc.psum_tensor(name, [P, 512], F32))

        def sem(name):
            return es.enter_context(nc.semaphore(name))

        w_hi = sb("w_hi", [P, NF * H], F32R)
        w_lo = sb("w_lo", [P, NF * H], F32R)
        w0_hi = sb("w0_hi", [P, NCH, H], F32R)
        w0_lo = sb("w0_lo", [P, NCH, H], F32R)
        outer = sb("outer", [P, NJ, B])
        outer_flat = outer[:, :, :].rearrange("p j b -> p (j b)")
        pairs = sb("pairs", [P, 2, TG, NPAIR])
        pairs_flat = pairs[:, :, :, :].rearrange("p a t n -> p (a t n)")
        pt_hi = sb("pt_hi", [P, 2, 512], F32R)
        pt_lo = sb("pt_lo", [P, 2, 512], F32R)
        x1_hi = sb("x1_hi", [P, 2, 512], F32R)
        x1_lo = sb("x1_lo", [P, 2, 512], F32R)
        scaled = sb("scaled", [P, 8, 512])
        sv = [scaled[:, i, :] for i in range(3)]
        sg = [scaled[:, 3 + i, :] for i in range(3)]
        gsum = [scaled[:, 6 + i, :] for i in range(2)]
        acc = sb("acc", [P, 512])
        acc2 = sb("acc2", [P, 256])
        x2 = sb("x2", [P, 2, H])
        rows = sb("rows", [P, 2, QF, D])
        emb_t = sb("emb_t", [P, 4, GB, D])
        emb_t_flat = emb_t[:, :, :, :].rearrange("p q b d -> p (q b d)")
        emb = sb("emb", [P, 2, TG, NJ])
        embs = sb("embs", [P, 2, TG, NJ])
        embd = sb("embd", [P, 2, TB, NJ])
        ids_sb = sb("ids_sb", [P, NIDX * QF], I32)
        first_sb = sb("first_sb", [P, QF], I32)
        idx = sb("idx", [P, 2, QF], I32)
        ident = sb("ident", [P, P])
        bmask = sb("bmask", [P, TB])
        z0 = sb("z0", [P, B])
        bias = sb("bias", [P, 16])

        y = [pb(f"y{i}") for i in range(YB)]
        scr = [pb(f"scr{i}") for i in range(2)]
        ps_x1 = pb("ps_x1")
        ps_g = pb("ps_g")

        s_ids = sem("s_ids")
        s_const = sem("s_const")
        s_w0 = sem("s_w0")
        s_w1 = sem("s_w1")
        s_w0sum = sem("s_w0sum")
        s_w0hi = sem("s_w0hi")
        s_w0lo = sem("s_w0lo")
        s_w1hi = sem("s_w1hi")
        s_w1lo = sem("s_w1lo")
        s_ones = sem("s_ones")
        s_idx = sem("s_idx")
        s_rows = [sem("s_rows0"), sem("s_rows1")]
        s_unit = sem("s_unit")
        s_unit_act = sem("s_unit_act")
        s_lo = sem("s_lo")
        s_pairs = sem("s_pairs")
        s_l0 = sem("s_l0")
        s_x1hi = sem("s_x1hi")
        s_x1 = sem("s_x1")
        s_embs = sem("s_embs")
        s_embd = sem("s_embd")
        s_y = sem("s_y")
        s_scaled = sem("s_scaled")
        s_gadd = sem("s_gadd")
        s_chain = sem("s_chain")
        s_outer = sem("s_outer")
        s_outer_sb = sem("s_outer_sb")
        s_w2 = sem("s_w2")
        s_top = sem("s_top")
        s_w2hi = sem("s_w2hi")
        s_w2lo = sem("s_w2lo")
        s_ohi = sem("s_ohi")
        s_olo = sem("s_olo")
        s_l2 = sem("s_l2")
        s_z = sem("s_z")
        s_part = sem("s_part")
        s_h1ps = sem("s_h1ps")
        s_h1 = sem("s_h1")
        s_h2ps = sem("s_h2ps")
        s_h2 = sem("s_h2")
        s_yps = sem("s_yps")
        s_ysb = sem("s_ysb")
        s_out = sem("s_out")
        s_pe_passed = sem("s_pe_passed")
        s_pool_passed = sem("s_pool_passed")

        w2_raw = pairs_flat[:, 0:NF * H]
        wt1_sb = pairs_flat[:, NF * H:NF * H + 3 * T1].rearrange("p (c n) -> p c n", c=3)
        wt1c_sb = pairs_flat[0:CTX, NF * H + 3 * T1:NF * H + 4 * T1]
        wt2_sb = emb_t_flat[:, 0:4 * T2].rearrange("p (c n) -> p c n", c=4)
        ctx_sb = emb_t_flat[0:CTX, 4 * T2:4 * T2 + B]
        w1_raw = outer_flat[:, 0:NF * H]
        w0a_raw = outer_flat[:, NF * H:NF * H + NCH * H]
        w0b_raw = outer_flat[:, NF * H + NCH * H:NF * H + 2 * NCH * H]
        w0s = outer_flat[:, NF * H + 2 * NCH * H:NF * H + 3 * NCH * H]
        w0_hi_f = w0_hi[:, :, :].rearrange("p c h -> p (c h)")
        w0_lo_f = w0_lo[:, :, :].rearrange("p c h -> p (c h)")
        b0_c, b2_c, b0x, b2x = (bias[:, i:i + 1] for i in range(4))
        N_PAIRS_ALL = (NG + 1) * TG

        def chunk_rows(c):
            return min(P, NPAIR - c * P)

        def fields_of(k):
            return FIELDS4[k] * 4, min(4, NF - FIELDS4[k] * 4)

        def unit_number(g, u):
            return u if g is None else count(g, NU, NPU + u)

        def unit_bank(g, u):
            return scr[u % 2] if g is None else scr[(NPU + NU + u) % 2]

        def chunk_number(g, c):
            return c if g is None else count(g, NCH, NCH + c)

        def seq(g):
            return PRO_UNITS if g is None else UNITS

        def prev_unit(g, u):
            if u >= 2:
                return g, u - 2
            if g is None:
                return None
            if isinstance(g, int) and g == 0:
                return None, NPU - 2 + u
            return g - 1, NU - 2 + u

        def chunks_before(units, u):
            return sum(e[0] == "T" for e in units[:u])

        def w2j_hi(i):
            return w0_hi[:, i, :]

        def w2j_lo(i):
            return w0_lo[:, i, :]

        def oj_hi(i):
            return [pt_hi[:, 0, :], pt_hi[:, 1, :], x1_hi[:, 0, :]][i]

        def oj_lo(i):
            return [pt_lo[:, 0, :], pt_lo[:, 1, :], x1_lo[:, 0, :]][i]

        def rows_count(g, par):
            if isinstance(g, int):
                return 16 * QF * (g // 2 + 2)
            return g * (8 * QF) + (-par + 4) * (8 * QF)

        block = es.enter_context(nc.Block())

        @block.sync
        def _(sp):
            sp.dma_start(ids_sb[:, :], ids).then_inc(s_ids, 16)
            sp.dma_start(first_sb[:, :], first_row).then_inc(s_ids, 16)
            sp.dma_start(ident[:, :], ident_in).then_inc(s_const, 16)
            sp.dma_start(bmask[:, :], bmask_in).then_inc(s_const, 16)
            sp.dma_start(bias[:, 0:1], b0).then_inc(s_const, 16)
            sp.dma_start(bias[:, 1:2], b2).then_inc(s_const, 16)
            sp.dma_start(bias[:, 4:8], bt1).then_inc(s_const, 16)
            sp.dma_start(bias[:, 8:10], bt2).then_inc(s_const, 16)
            sp.dma_start(bias[:, 10:12], wt3).then_inc(s_const, 16)
            sp.dma_start(sg[1][:, 3 * H:4 * H], b1.broadcast_to((P, H))).then_inc(s_const, 16)
            sp.dma_start(w0a_raw, w0a).then_inc(s_w0, 16)
            sp.dma_start(w0b_raw, w0b).then_inc(s_w0, 16)
            sp.dma_start(w1_raw, w1).then_inc(s_w1, 16)
            sp.wait_ge(s_pairs, N_PAIRS_ALL)
            sp.wait_ge(s_unit, NPU + NU * (NG - 1))
            sp.dma_start(w2_raw, w2).then_inc(s_w2, 16)
            sp.dma_start(wt1_sb, wt1).then_inc(s_top, 16)
            sp.dma_start(wt1c_sb, wt1c).then_inc(s_top, 16)
            sp.dma_start(wt2_sb, wt2).then_inc(s_top, 16)
            sp.dma_start(ctx_sb, ctx_t).then_inc(s_top, 16)
            sp.wait_ge(s_ysb, 1)
            sp.dma_start(out, acc[0:1, 0:B]).then_inc(s_out, 16)
            sp.wait_ge(s_out, 16)

        @block.tensor
        def _(pe):
            def free_unit(g, u):
                before = prev_unit(g, u)
                if before is None:
                    return
                bg, bu = before
                if seq(bg)[bu][0] == "T":
                    pe.wait_ge(s_lo, chunk_number(bg, chunks_before(seq(bg), bu)) + 1)
                else:
                    pe.wait_ge(s_unit_act, unit_number(bg, bu) + 1)

            def step_e(g, u, k, par, rows_wait):
                free_unit(g, u)
                ps = unit_bank(g, u)
                if k == 0:
                    pe.wait_ge(s_rows[par], rows_wait)
                if k < 4:
                    for i in range(4):
                        last = nc.tensor.transpose(ps[0:QF, i * P:(i + 1) * P], rows[:, par, :, 4 * k + i],
                                                   ident[:, :])
                else:
                    pe.wait_ge(s_unit_act, unit_number(g, u - UNIT_BACK(g, u)) + 1)
                    pe.sem_inc(s_pe_passed)
                    for t in range(TG):
                        for q in range(4):
                            last = nc.tensor.transpose(
                                ps[:, t * NJ + q * QF:t * NJ + (q + 1) * QF],
                                emb_t[0:QF, q, t * TB:(t + 1) * TB, :].rearrange("p b d -> p (b d)"),
                                ident[0:QF, 0:QF])
                last.then_inc(s_unit, 1)

            def UNIT_BACK(g, u):
                return next(n for n in range(1, u + 1) if seq(g)[u - n] == ("E", 3))

            def step_t(g, u, c, par, pairs_wait):
                free_unit(g, u)
                ps = unit_bank(g, u)
                if c == 0:
                    pe.wait_ge(s_pairs, pairs_wait)
                n = chunk_rows(c)
                for t in range(TG):
                    last = nc.tensor.transpose(ps[0:n, t * P:(t + 1) * P], pairs[:, par, t, c * P:c * P + n],
                                               ident[:, :])
                last.then_inc(s_unit, 1)

            def step_m(g, c, x1_free):
                pe.wait_ge(s_lo, chunk_number(g, c) + 1)
                if c == 0 and x1_free is not None:
                    pe.wait_ge(s_x1, x1_free)
                n, r = chunk_rows(c), c % 2
                nc.tensor.matmul(ps_x1[:, :], w0_hi[0:n, c, :], pt_hi[0:n, r, :], start=(c == 0), stop=False)
                nc.tensor.matmul(ps_x1[:, :], w0_lo[0:n, c, :], pt_hi[0:n, r, :], start=False, stop=False)
                nc.tensor.matmul(ps_x1[:, :], w0_hi[0:n, c, :], pt_lo[0:n, r, :], start=False,
                                 stop=(c == NCH - 1)).then_inc(s_l0, 1)

            def outer_products(g, t):
                n = count(g, TG, t)
                pe.wait_ge(s_chain, count(g, TG * CHAIN, (t + 1) * CHAIN))
                pe.wait_ge(s_embd, n + 1)
                if not (isinstance(n, int) and n == 0):
                    pe.wait_ge(s_outer_sb, n)
                nc.tensor.matmul(ps_g[:, 0:TB * NJ], x2[:, t % 2, :],
                                 embd[:, t % 2, :, :].rearrange("p b j -> p (b j)"),
                                 start=True, stop=True).then_inc(s_outer, 1)

            def body(g, par, first=False, last=False):
                for s in range(NS):
                    t, k = divmod(s, NBK)
                    for what, i in EXTRA.get(s, []):
                        u = UNITS.index((what, i)) if what != "M" else None
                        if last:
                            continue
                        if what == "T":
                            step_t(g, u, i, 1 - par, count(g, TG, 2 * TG))
                        elif what == "E":
                            step_e(g, u, i, par, rows_count(g, par))
                        else:
                            step_m(g, i, count(g, 2, 2))
                    if k == G_SLOT and (t or not first):
                        outer_products(g if t else g - 1, (t - 1) % TG)
                    if s == 0:
                        pe.wait_ge(s_x1, count(g, 2, 1))
                    if not (first and s < YB):
                        tb, kb = divmod((s - YB) % NS, NBK)
                        gb = g if s >= YB else g - 1
                        if KIND[kb] == "D":
                            pe.wait_ge(s_chain, count(gb, TG * CHAIN, tb * CHAIN + CHAIN_AFTER[kb]))
                        else:
                            n = sum(KIND[i] != "D" for i in range(kb + 1))
                            pe.wait_ge(s_scaled, count(gb, TG * N_ACT, tb * N_ACT + n))
                    f, m = fields_of(k)
                    o = y[s % YB][:, 0:m * H]
                    if first and t == 0:
                        pe.wait_ge(s_w1lo, FIELDS4[k] + 1)
                    hi = x1_hi[:, par, t * P:(t + 1) * P]
                    lo = x1_lo[:, par, t * P:(t + 1) * P]
                    nc.tensor.matmul(o, hi, w_hi[:, f * H:(f + m) * H], start=True, stop=False)
                    nc.tensor.matmul(o, hi, w_lo[:, f * H:(f + m) * H], start=False, stop=False)
                    nc.tensor.matmul(o, lo, w_hi[:, f * H:(f + m) * H], start=False, stop=True).then_inc(s_y, 1)

            pe.wait_ge(s_const, 8 * 16)
            for u, (what, i) in enumerate(PRO_UNITS):
                if what == "E":
                    n = u // 5
                    step_e(None, u, i, n, 16 * QF)
                else:
                    if i == 0:
                        pe.wait_ge(s_w0lo, 1)
                    step_t(None, u, i, 0, TG)
                    if i:
                        step_m(None, i - 1, None)
            step_m(None, NCH - 1, None)
            body(0, 0, first=True)
            with pe.Fori(0, NG // 2 - 1) as pair:
                body(pair * 2 + 1, 1)
                body(pair * 2 + 2, 0)
            body(NG - 1, 1, last=True)
            outer_products(NG - 1, TG - 1)

            pe.wait_ge(s_top, 4 * 16)
            pe.wait_ge(s_outer_sb, NG * TG)
            pe.wait_ge(s_z, 1)
            for m in range(4):
                o, c = y[m][:, :], slice(m * P, (m + 1) * P)
                nc.tensor.matmul(o, wt1_sb[:, 0, c], scaled[:, 4, :], start=True, stop=False)
                nc.tensor.matmul(o, wt1_sb[:, 1, c], outer[:, NF, :], start=False, stop=False)
                nc.tensor.matmul(o, wt1c_sb[:, c], ctx_sb, start=False, stop=False).then_inc(s_part, 1)
            def fields3(j, start=False, stop=False):
                for i in range(3):
                    pe.wait_ge(s_w2lo, j + (i + 1))
                    pe.wait_ge(s_olo, j + (i + 1))
                    nc.tensor.matmul(ps_x1[:, :], w2j_hi(i), oj_hi(i), start=start and i == 0, stop=False)
                    nc.tensor.matmul(ps_x1[:, :], w2j_lo(i), oj_hi(i), start=False, stop=False)
                    nc.tensor.matmul(ps_x1[:, :], w2j_hi(i), oj_lo(i), start=False,
                                     stop=stop and i == 2).then_inc(s_l2, 1)

            fields3(0, start=True)
            with pe.Fori(1, NF // 3 - 1) as three:
                fields3(three * 3)
            fields3(NF - 3, stop=True)
            pe.wait_ge(s_z, 2)
            for m in range(4):
                nc.tensor.matmul(y[m][:, :], wt1_sb[:, 2, m * P:(m + 1) * P], scaled[:, 5, :], start=False,
                                 stop=True).then_inc(s_h1ps, 1)
            for m in range(2):
                for c in range(4):
                    pe.wait_ge(s_h1, c + 1)
                    last = nc.tensor.matmul(scr[m][:, :], wt2_sb[:, c, m * P:(m + 1) * P], scaled[:, c, :],
                                            start=(c == 0), stop=(c == 3))
                last.then_inc(s_h2ps, 1)
            for c in range(2):
                pe.wait_ge(s_h2, c + 1)
                last = nc.tensor.matmul(ps_g[0:1, :], bias[:, 10 + c:11 + c], scaled[:, 6 + c, :],
                                        start=(c == 0), stop=(c == 1))
            last.then_inc(s_yps, 1)

        @block.scalar
        def _(act):
            def unit(g, u, what, i, par):
                act.wait_ge(s_unit, unit_number(g, u) + 1)
                ps = unit_bank(g, u)
                if what == "T":
                    n = chunk_number(g, i)
                    if not (isinstance(n, int) and n < 2):
                        act.wait_ge(s_l0, n - (1 if i >= 2 else i))
                    r = chunk_rows(i)
                    nc.scalar.copy(pt_hi[0:r, i % 2, :], ps[0:r, :]).then_inc(s_unit_act, 1)
                elif i < 4:
                    nc.scalar.copy(
                        emb_t[0:QF, :, :, 4 * i:4 * i + 4].rearrange("p q b d -> p d (q b)"),
                        ps[0:QF, :].rearrange("p (d n) -> p d n", d=4)).then_inc(s_unit_act, 1)
                else:
                    if g is not None:
                        act.wait_ge(s_embs, count(g, 1, 1))
                    nc.scalar.copy(emb[:, par, :, :].rearrange("p t j -> p (t j)"),
                                   ps[:, 0:TG * NJ]).then_inc(s_unit_act, 1)

            def x1_high(g, par, chunks, y_before):
                act.wait_ge(s_l0, chunks)
                if y_before is not None:
                    act.wait_ge(s_y, y_before)
                nc.scalar.activation(x1_hi[:, par, :], ps_x1[:, :], ACT.Identity, bias=b0_c,
                                     scale=1.0).then_inc(s_x1hi, 1)

            def outer_out(g, t):
                n = count(g, TG, t)
                act.wait_ge(s_outer, n + 1)
                nc.scalar.copy(outer[:, :, bass.ds(n * TB, TB)],
                               ps_g[:, 0:TB * NJ].rearrange("p (b j) -> p j b", b=TB)).then_inc(s_outer_sb, 1)

            def body(g, par, first=False, last=False):
                for s in range(NS):
                    t, k = divmod(s, NBK)
                    for what, i in EXTRA.get(s, []):
                        if not last and what != "M":
                            unit(g, UNITS.index((what, i)), what, i, par)
                    if s == X1_SLOT + 1 and not last:
                        x1_high(g, 1 - par, count(g, NCH, 2 * NCH), count(g, NS, 0) if not first else None)
                    if k == G_SLOT + 1 and (t or not first):
                        outer_out(g if t else g - 1, (t - 1) % TG)
                    if KIND[k] == "D":
                        continue
                    if s == 0:
                        act.wait_ge(s_embs, count(g, 1, 1))
                    act.wait_ge(s_y, count(g, NS, s + 1))
                    f, m = fields_of(k)
                    fresh = first and t == 0
                    if KIND[k] == "V":
                        v = V_SLOTS.index(k)
                        dst = sv[v]
                        if not fresh:
                            after = CHAIN_AFTER[2] if v == 0 else CHAIN_AFTER[k]
                            act.wait_ge(s_chain, count(g, TG * CHAIN, (t - 1) * CHAIN + after))
                    else:
                        v = G_SLOTS.index(k)
                        dst = sg[v]
                        if not fresh:
                            act.wait_ge(s_gadd, count(g, TG * 2, (t - 1) * 2 + (1 if v < 2 else 2)))
                    for i in range(m):
                        last_i = nc.scalar.mul(dst[:, i * H:(i + 1) * H], y[s % YB][:, i * H:(i + 1) * H],
                                               embs[:, par, t, f + i:f + i + 1])
                    last_i.then_inc(s_scaled, 1)

            act.wait_ge(s_const, 8 * 16)
            nc.scalar.mul(bias[:, 2:4], bias[:, 0:2], float(D))
            act.wait_ge(s_w0sum, 1)
            nc.scalar.copy(w0_hi_f, w0s).then_inc(s_w0hi, 1)
            act.wait_ge(s_w1, 16)
            for n in range(NBK):
                c = slice(n * 512, min((n + 1) * 512, NF * H))
                nc.scalar.copy(w_hi[:, c], w1_raw[:, c]).then_inc(s_w1hi, 1)
            for u, (what, i) in enumerate(PRO_UNITS):
                unit(None, u, what, i, u // 5 if what == "E" else 0)
            x1_high(None, 0, NCH, None)
            body(0, 0, first=True)
            with act.Fori(0, NG // 2 - 1) as pair:
                body(pair * 2 + 1, 1)
                body(pair * 2 + 2, 0)
            body(NG - 1, 1, last=True)
            outer_out(NG - 1, TG - 1)

            act.wait_ge(s_x1, 2 * NG)
            act.wait_ge(s_gadd, 2 * NG * TG)
            nc.scalar.activation(scaled[:, 4, :], z0[:, :], ACT.Identity, bias=b0x, scale=1.0).then_inc(s_z, 1)
            def high3(j, first=False):
                for i in range(3):
                    if not first:
                        act.wait_ge(s_l2, j + (i - 2))
                    nc.scalar.copy(oj_hi(i), outer_flat[:, bass.ds((j + i) * B, B)]).then_inc(s_ohi, 1)

            act.wait_ge(s_outer_sb, NG * TG)
            act.wait_ge(s_l0, NCH * NG)
            act.wait_ge(s_y, NS * NG)
            high3(0, first=True)
            with act.Fori(1, NF // 3) as three:
                high3(three * 3)
            act.wait_ge(s_l2, NF)
            nc.scalar.activation(scaled[:, 5, :], ps_x1[:, :], ACT.Identity, bias=b2x, scale=1.0).then_inc(s_z, 1)
            for m in range(4):
                act.wait_ge(s_h1ps, m + 1)
                nc.scalar.activation(scaled[:, m, :], y[m][:, :], ACT.Relu, bias=bias[:, 4 + m:5 + m],
                                     scale=1.0).then_inc(s_h1, 1)
            for m in range(2):
                act.wait_ge(s_h2ps, m + 1)
                nc.scalar.activation(scaled[:, 6 + m, :], scr[m][:, :], ACT.Relu, bias=bias[:, 8 + m:9 + m],
                                     scale=1.0).then_inc(s_h2, 1)
            act.wait_ge(s_yps, 1)
            nc.scalar.copy(acc[0:1, 0:B], ps_g[0:1, :]).then_inc(s_ysb, 1)

        def tile_pairs(eng, par, t):
            at = 0
            for a, m in FBLOCKS:
                n = NF - a
                last = eng.tensor_tensor(
                    pairs[:, par, t, at:at + m * n].rearrange("p (j k) -> p j k", j=m),
                    emb[:, par, t, a:a + m].unsqueeze(2).broadcast_to((P, m, n)),
                    emb[:, par, t, a:NF].unsqueeze(1).broadcast_to((P, m, n)), ALU.mult)
                at += m * n
            return last

        @block.vector
        def _(dve):
            def chunk_low(g, c, u):
                dve.wait_ge(s_unit_act, unit_number(g, u) + 1)
                r = chunk_rows(c)
                nc.vector.tensor_tensor(pt_lo[0:r, c % 2, :], unit_bank(g, u)[0:r, :],
                                        pt_hi[0:r, c % 2, :].bitcast(F32), ALU.subtract).then_inc(s_lo, 1)

            def x1_low(g1, par):
                dve.wait_ge(s_x1hi, count(g1, 1, 1))
                nc.vector.scalar_tensor_tensor(out=x1_lo[:, par, :], in0=ps_x1[:, :], scalar=b0_c,
                                               in1=x1_hi[:, par, :].bitcast(F32), op0=ALU.add,
                                               op1=ALU.subtract).then_inc(s_x1, 1)
                nc.vector.reduce_sum(z0[:, bass.ds(g1 * GB, GB)],
                                     ps_x1[:, :].rearrange("p (b d) -> p b d", d=D),
                                     axis=AX.X).then_inc(s_x1, 1)

            def body(g, par, first=False, last=False):
                for s in range(NS):
                    t, k = divmod(s, NBK)
                    base = t * CHAIN

                    def chained(n):
                        v = count(g, TG * CHAIN, base + n)
                        if not (isinstance(v, int) and v == 0):
                            dve.wait_ge(s_chain, v)

                    for what, i in EXTRA.get(s - 1, []):
                        if not last and what == "T":
                            chunk_low(g, i, UNITS.index((what, i)))
                    if s == X1_SLOT + 2 and not last:
                        x1_low(g + 1, 1 - par)
                    if s == 0:
                        dve.wait_ge(s_embs, count(g, 1, 1))
                    f, m = fields_of(k)
                    n = CHAIN_AFTER[k]
                    if KIND[k] == "D":
                        dve.wait_ge(s_y, count(g, NS, s + 1))
                        if k == 2:
                            dve.wait_ge(s_scaled, count(g, TG * N_ACT, t * N_ACT + 1))
                        for i in range(m):
                            b = slice(i * H, (i + 1) * H)
                            if k == 2:
                                if i == 0:
                                    chained(0)
                            else:
                                before = [q for q in range(k) if KIND[q] != "G"][-1]
                                chained(n - m if KIND[before] == "V" else n - m + i - 3)
                            nc.vector.scalar_tensor_tensor(
                                out=acc[:, b], in0=y[s % YB][:, b], scalar=embs[:, par, t, f + i:f + i + 1],
                                in1=sv[0][:, b] if k == 2 else acc[:, b],
                                op0=ALU.mult, op1=ALU.add).then_inc(s_chain, 1)
                    elif KIND[k] == "V" and k:
                        a = sum(KIND[i] != "D" for i in range(k + 1))
                        dve.wait_ge(s_scaled, count(g, TG * N_ACT, t * N_ACT + a))
                        chained(n - 1)
                        nc.vector.tensor_tensor(acc[:, :], acc[:, :], sv[V_SLOTS.index(k)],
                                                ALU.add).then_inc(s_chain, 1)
                    if k == NBK - 1:
                        dve.wait_ge(s_gadd, count(g, TG * 2, t * 2 + 2))
                        chained(FOLD_IN)
                        nc.vector.tensor_tensor(acc[:, :], acc[:, :], gsum[1], ALU.add).then_inc(s_chain, 1)
                        chained(FOLD_IN + 1)
                        nc.vector.tensor_tensor(acc2[:, :], acc[:, 0:256], acc[:, 256:512],
                                                ALU.add).then_inc(s_chain, 1)
                        chained(FOLD_IN + 2)
                        tile_before = count(g, TG, t - 1)
                        if not (isinstance(tile_before, int) and tile_before <= 0):
                            dve.wait_ge(s_outer, tile_before)
                        nc.vector.tensor_tensor(x2[:, t % 2, :], acc2[:, 0:H], acc2[:, H:2 * H],
                                                ALU.add).then_inc(s_chain, 1)

            dve.wait_ge(s_w0, 32)
            nc.vector.tensor_tensor(w0s, w0a_raw, w0b_raw, ALU.add).then_inc(s_w0sum, 1)
            dve.wait_ge(s_w0hi, 1)
            nc.vector.tensor_tensor(w0_lo_f, w0s, w0_hi_f.bitcast(F32), ALU.subtract).then_inc(s_w0lo, 1)
            for n in range(NBK):
                dve.wait_ge(s_w1hi, n + 1)
                c = slice(n * 512, min((n + 1) * 512, NF * H))
                nc.vector.tensor_tensor(w_lo[:, c], w1_raw[:, c], w_hi[:, c].bitcast(F32),
                                        ALU.subtract).then_inc(s_w1lo, 1)
            for g0 in range(2):
                dve.wait_ge(s_unit_act, 5 * (g0 + 1))
                for t in range(TG):
                    tile_pairs(nc.vector, g0, t).then_inc(s_pairs, 1)
            for c in range(NCH):
                chunk_low(None, c, 10 + c)
            x1_low(0, 0)
            body(0, 0, first=True)
            with dve.Fori(0, NG // 2 - 1) as pair:
                body(pair * 2 + 1, 1)
                body(pair * 2 + 2, 0)
            body(NG - 1, 1, last=True)
            with dve.Fori(0, NF // 3) as three:
                j = three * 3
                for i in range(3):
                    dve.wait_ge(s_ohi, j + (i + 1))
                    nc.vector.tensor_tensor(oj_lo(i), outer_flat[:, bass.ds((j + i) * B, B)],
                                            oj_hi(i).bitcast(F32), ALU.subtract).then_inc(s_olo, 1)

        @block.gpsimd
        def _(pool):
            def row_numbers(g3, par):
                pool.sem_inc(s_pool_passed)
                nc.gpsimd.tensor_tensor(idx[:, par, :], ids_sb[:, bass.ds(g3 * QF, QF)], first_sb[:, :],
                                        ALU.add).then_inc(s_idx, 1)

            def gather(par, i):
                nc.gpsimd.indirect_dma_start(
                    out=rows[:, par, i, :], out_offset=None, in_=table,
                    in_offset=bass.IndirectOffsetOnAxis(ap=idx[:, par, i:i + 1], axis=0)).then_inc(s_rows[par], 16)

            def copy_embs(par):
                pool.sem_inc(s_pool_passed)
                nc.gpsimd.tensor_copy(embs[:, par, :, 0:NF], emb[:, par, :, 0:NF]).then_inc(s_embs, 1)

            def block_diagonal(g, par, t):
                n = count(g, TG, t)
                if not (isinstance(n, int) and n < 2):
                    pool.wait_ge(s_outer, n - 1)
                nc.gpsimd.tensor_tensor(embd[:, t % 2, :, :],
                                        embs[:, par, t, :].unsqueeze(1).broadcast_to((P, TB, NJ)),
                                        bmask[:, :].unsqueeze(2).broadcast_to((P, TB, NJ)),
                                        ALU.mult).then_inc(s_embd, 1)

            def add(g, t, which, first):
                slot = G_SLOTS[which + 1]
                a = sum(KIND[i] != "D" for i in range(slot + 1))
                pool.wait_ge(s_scaled, count(g, TG * N_ACT, t * N_ACT + a))
                if which == 0:
                    if not (first and t == 0):
                        pool.wait_ge(s_gadd, count(g, TG * 2, t * 2))
                    nc.gpsimd.tensor_tensor(gsum[0], sg[0], sg[1], ALU.add).then_inc(s_gadd, 1)
                else:
                    pool.wait_ge(s_gadd, count(g, TG * 2, t * 2 + 1))
                    if not (first and t == 0):
                        pool.wait_ge(s_chain, count(g, TG * CHAIN, (t - 1) * CHAIN + FOLD_IN + 1))
                    nc.gpsimd.tensor_tensor(gsum[1], gsum[0], sg[2], ALU.add).then_inc(s_gadd, 1)

            def body(g, par, first=False, last=False):
                if first:
                    pool.wait_ge(s_unit_act, 10)
                if not last:
                    if not first:
                        pool.wait_ge(s_scaled, count(g, TG * N_ACT, 0))
                        pool.wait_ge(s_chain, count(g, TG * CHAIN, FOLD_IN - CHAIN))
                    copy_embs(1 - par)
                pool.wait_ge(s_embs, count(g, 1, 1))
                for t in range(TG):
                    block_diagonal(g, par, t)
                    if not last:
                        if t == 0:
                            n = unit_number(g - 1, UNITS.index(("E", 3))) + 1 if not first else 9
                            pool.wait_ge(s_unit, n)
                            row_numbers(g + 3, 1 - par)
                            pool.wait_ge(s_idx, count(g, 1, 4))
                            pool.sem_inc(s_pool_passed)
                        for i in [[0, 1, 2], [5, 6], [8], []][t]:
                            gather(1 - par, i)
                        if t in (1, 2, 3):
                            if t == 1:
                                pool.wait_ge(s_unit_act, unit_number(g, UNITS.index(("E", 4))) + 1)
                                n = unit_number(g - 1, UNITS.index(("T", 6))) + 1 if not first else NPU
                                pool.wait_ge(s_unit, n)
                            tile_pairs(nc.gpsimd, par, t - 1).then_inc(s_pairs, 1)
                    add(g, t, 0, first)
                    if not last:
                        for i in [[3, 4], [7], [9], []][t]:
                            gather(1 - par, i)
                    add(g, t, 1, first)
                    if t == 3 and not last:
                        tile_pairs(nc.gpsimd, par, 3).then_inc(s_pairs, 1)

            nc.gpsimd.memset(embs[:, :, :, NF:NJ], 1.0).then_inc(s_ones, 1)
            pool.wait_ge(s_ids, 32)
            for g0 in range(3):
                if g0 == 2:
                    pool.wait_ge(s_unit, 4)
                row_numbers(g0, g0 % 2)
                pool.wait_ge(s_idx, g0 + 1)
                for i in range(QF):
                    gather(g0 % 2, i)
                if g0 == 1:
                    pool.wait_ge(s_ones, 1)
                    pool.wait_ge(s_const, 8 * 16)
                    pool.wait_ge(s_unit_act, 5)
                    copy_embs(0)
            body(0, 0, first=True)
            with pool.Fori(0, NG // 2 - 1) as pair:
                body(pair * 2 + 1, 1)
                body(pair * 2 + 2, 0)
            body(NG - 1, 1, last=True)
            pool.wait_ge(s_rows[0], 16 * QF * (NIDX // 2))
            pool.wait_ge(s_rows[1], 16 * QF * (NIDX // 2))
            pool.wait_ge(s_w2, 16)
            pool.wait_ge(s_l0, NCH * NG)

            def weights3(j, first=False):
                for i in range(3):
                    if not first:
                        pool.wait_ge(s_l2, j + (i - 2))
                    pool.sem_inc(s_pool_passed)
                    nc.gpsimd.tensor_copy(w2j_hi(i), w2_raw[:, bass.ds((j + i) * H, H)]).then_inc(s_w2hi, 1)
                    pool.wait_ge(s_w2hi, j + (i + 1))
                    pool.sem_inc(s_pool_passed)
                    nc.gpsimd.tensor_tensor(w2j_lo(i), w2_raw[:, bass.ds((j + i) * H, H)],
                                            w2j_hi(i).bitcast(F32), ALU.subtract).then_inc(s_w2lo, 1)

            weights3(0, first=True)
            with pool.Fori(1, NF // 3) as three:
                weights3(three * 3)


def _layout(inputs):
    a = {k: np.asarray(v) for k, v in inputs.items()}
    table = np.concatenate([a[f"tbl_{f}"] for f in range(NF)], axis=0)
    ids = np.zeros((NIDX * GB, NJ), a["ids"].dtype)
    ids[0:B, 0:NF] = a["ids"]
    ids = ids.reshape(NIDX, GB, 4, QF).transpose(2, 1, 0, 3).reshape(P, NIDX * QF)
    first = np.zeros(NJ, np.int32)
    first[0:NF] = np.cumsum([0] + VOCAB[:-1])
    first_row = np.repeat(first.reshape(4, 1, QF), GB, axis=1).reshape(P, QF)
    ident = np.eye(P, dtype=np.float32)
    bmask = np.repeat(np.eye(TB, dtype=np.float32), D, axis=0)
    w0 = a["L0_rec_W0"].reshape(H, NF, NF)
    w0a = np.zeros((NCH * P, H), w0.dtype)
    w0b = np.zeros((NCH * P, H), w0.dtype)
    at = 0
    for f, m in FBLOCKS:
        n = NF - f
        w0a[at:at + m * n] = w0[:, f:f + m, f:].reshape(H, m * n).T
        other = w0[:, f:, f:f + m].transpose(2, 1, 0).copy()
        other[:, 0:m] = 0
        w0b[at:at + m * n] = other.reshape(m * n, H)
        at += m * n

    def chunks(x, n):
        return x.reshape(n, P, -1).transpose(1, 0, 2)

    def by_field(w):
        return w.reshape(H, NF, H).transpose(2, 1, 0).reshape(H, NF * H)

    return [
        ("table", table), ("ids_g", ids), ("first_row", first_row), ("ident_c", ident), ("bmask_c", bmask),
        ("w0a", chunks(w0a, NCH).reshape(P, NCH * H)), ("w0b", chunks(w0b, NCH).reshape(P, NCH * H)),
        ("w1", by_field(a["L0_rec_W1"])), ("w2", by_field(a["L0_rec_W2"])),
        ("b0", a["L0_rec_b0"].reshape(P, 1)), ("b1", a["L0_rec_b1"].reshape(1, H)),
        ("b2", a["L0_rec_b2"].reshape(P, 1)),
        ("wt1", chunks(a["W_top1"][0:3 * H], 3)), ("wt1c", a["W_top1"][3 * H:]),
        ("bt1", a["b_top1"].reshape(4, P).T), ("wt2", chunks(a["W_top2"], 4)),
        ("bt2", a["b_top2"].reshape(2, P).T), ("wt3", a["W_top3"].reshape(2, P).T),
        ("ctx_t", a["dense_ctx"].T),
    ]


def kernel(**inputs):
    import concourse.bacc as bacc
    from concourse.bass_utils import run_bass_kernel_spmd

    nc = bacc.Bacc("TRN2", target_bir_lowering=False, num_devices=1)
    arrays, args = {}, []
    for name, a in _layout(inputs):
        a = np.ascontiguousarray(a)
        arrays[f"in_{name}"] = a
        args.append(nc.dram_tensor(f"in_{name}", a.shape, mybir.dt.from_np(a.dtype), kind="ExternalInput").ap())
    res = nc.dram_tensor("out_0", (1, B), F32, kind="ExternalOutput").ap()
    build(nc, *args, res)
    r = run_bass_kernel_spmd(nc, [arrays], core_ids=[0])
    return r.results[0]["out_0"].reshape(B, 1)
```

```python
import concourse.bass as bass
from concourse import mybir
from contextlib import ExitStack
import numpy as np

F32 = mybir.dt.float32
F32R = mybir.dt.float32r
I32 = mybir.dt.int32
ALU = mybir.AluOpType
ACT = mybir.ActivationFunctionType
AX = mybir.AxisListType

VOCAB = [1250, 1250, 1000, 12500, 125000, 1250, 1000, 12500, 12500, 125000, 125000, 125000, 12500,
         125000, 1250, 1250, 1000, 125000, 1000, 1250, 12500, 125000, 1000, 125000, 1000, 12500, 1000,
         1000, 12500, 1250, 1250, 125000, 1000, 1000, 1250, 1250, 1000, 1250, 1250]
B, NF, D, H = 512, 39, 16, 128
CTX = 16
T1, T2 = 512, 256
P = 128

TB = P // D
TG = 4
GB = TB * TG
NG = B // GB
NJ = 40
QF = NJ // 4
NCH = 7
FBLOCKS = [(0, 7), (7, 7), (14, 7), (21, 6), (27, 6), (33, 6)]
NPAIR = sum(m * (NF - a) for a, m in FBLOCKS)
assert (NCH - 1) * P < NPAIR <= NCH * P
NBK = 10
NS = TG * NBK
YB = 4

KIND = "VGGDVDGDVD"
FIELDS4 = [2, 1, 9, 3, 0, 4, 5, 6, 7, 8]
LAST4 = FIELDS4.index(9)
D_SLOTS, V_SLOTS, G_SLOTS = ([k for k in range(NBK) if KIND[k] == x] for x in "DVG")
assert len(V_SLOTS) == 3 and len(G_SLOTS) == 3 and LAST4 in G_SLOTS[0:2]
N_ACT = len(V_SLOTS) + len(G_SLOTS)
STEPS = [(3, 3), (5, 5), (7, 7), (9, 9), ('V', 9), ('G', 9), ('A', 9), ('F', 9), ('H', 9)]
DONE, n = {}, 0
for what, _ in STEPS:
    n += 4 if what in D_SLOTS else 1
    DONE[what] = n
CHAIN = n

PE_AT = {("T", 0): 3, ("T", 1): 5, ("T", 2): 12, ("T", 3): 13, ("T", 4): 17, ("T", 5): 20, ("T", 6): 23, ("E", 0): 0, ("E", 1): 7, ("E", 2): 9, ("E", 3): 16, ("E", 4): 18, ("M", 0): 9, ("M", 1): 14, ("M", 2): 17, ("M", 3): 21, ("M", 4): 22, ("M", 5): 31, ("M", 6): 32}
ACT_LEAD = 1
DVE_LAG = 0
X1_ACT, X1_DVE = 35, 36


POOL_AT = {("copy", 0): 3.2}
POOL_AT |= {("gather", i): [0, 1, 1, 4, 7, 11, 11, 13, 17, 19][i] for i in range(QF)}
POOL_AT |= {("pairs", t): [21, 28, 35, 37][t] for t in range(TG)}
POOL_AT |= {("diagonal", t): t * NBK + [13.1, 14.1, 11.1, 17.1][t] for t in range(TG)}
POOL_AT |= {("add", 2 * t + w): t * NBK + [8.5, 9.5][w] for t in range(TG) for w in range(2)}


def extras(shift=0, kinds="TEM"):
    at = {}
    for (what, i), s in sorted(PE_AT.items(), key=lambda x: x[1]):
        if what in kinds:
            at.setdefault(max(0, s + shift), []).append((what, i))
    return at


PE_EXTRA, ACT_EXTRA, DVE_EXTRA = extras(), extras(-ACT_LEAD, "TE"), extras(DVE_LAG, "T")
G_ACT = 5
G_SLOT = 7
UNITS = [e for s in range(NS) for e in PE_EXTRA.get(s, []) if e[0] in "TE"]
NU = len(UNITS)
PRO_UNITS = [("E", k) for k in range(5)] * 2 + [("T", c) for c in range(NCH)]
NPU = len(PRO_UNITS)
NIDX = NG + 2


def count(g, per_group, within):
    return g * per_group + within


def build(nc, table, ids, first_row, ident_in, bmask_in, w0a, w0b, w1, w2, b0, b1, b2,
          wt1, wt1c, bt1, wt2, bt2, wt3, ctx_t, out):
    es = ExitStack()
    with es:
        def sb(name, shape, dt=F32):
            return es.enter_context(nc.sbuf_tensor(name, shape, dt))

        def pb(name):
            return es.enter_context(nc.psum_tensor(name, [P, 512], F32))

        def sem(name):
            return es.enter_context(nc.semaphore(name))

        w_hi = sb("w_hi", [P, NF * H], F32R)
        w_lo = sb("w_lo", [P, NF * H], F32R)
        w0_hi = sb("w0_hi", [P, NCH, H], F32R)
        w0_lo = sb("w0_lo", [P, NCH, H], F32R)
        outer = sb("outer", [P, NJ, B])
        outer_flat = outer[:, :, :].rearrange("p j b -> p (j b)")
        pairs = sb("pairs", [P, 2, TG, NPAIR])
        pairs_flat = pairs[:, :, :, :].rearrange("p a t n -> p (a t n)")
        pt_hi = sb("pt_hi", [P, 2, 512], F32R)
        pt_lo = sb("pt_lo", [P, 2, 512], F32R)
        x1_hi = sb("x1_hi", [P, 2, 512], F32R)
        x1_lo = sb("x1_lo", [P, 2, 512], F32R)
        scaled = sb("scaled", [P, 8, 512])
        sv = [scaled[:, i, :] for i in range(3)]
        sg = [scaled[:, 3 + i, :] for i in range(3)]
        gsum = [scaled[:, 6 + i, :] for i in range(2)]
        acc = sb("acc", [P, 512])
        acc_b = sb("acc_b", [P, 512])
        x2 = sb("x2", [P, 2, H])
        rows = sb("rows", [P, 2, QF, D])
        emb_t = sb("emb_t", [P, 4, GB, D])
        emb_t_flat = emb_t[:, :, :, :].rearrange("p q b d -> p (q b d)")
        emb = sb("emb", [P, 2, TG, NJ])
        embs = sb("embs", [P, 2, TG, NJ])
        embd = sb("embd", [P, TB, NJ])
        ids_sb = sb("ids_sb", [P, NIDX * QF], I32)
        first_sb = sb("first_sb", [P, QF], I32)
        idx = sb("idx", [P, 2, QF], I32)
        ident = sb("ident", [P, P])
        bmask = sb("bmask", [P, TB])
        z0 = sb("z0", [P, B])
        bias = sb("bias", [P, 16])

        y = [pb(f"y{i}") for i in range(YB)]
        scr = [pb(f"scr{i}") for i in range(2)]
        ps_x1 = pb("ps_x1")
        ps_g = pb("ps_g")

        s_ids = sem("s_ids")
        s_const = sem("s_const")
        s_w0 = sem("s_w0")
        s_w1 = sem("s_w1")
        s_w0sum = sem("s_w0sum")
        s_w0hi = sem("s_w0hi")
        s_w0lo = sem("s_w0lo")
        s_w1hi = sem("s_w1hi")
        s_w1lo = sem("s_w1lo")
        s_ones = sem("s_ones")
        s_idx = sem("s_idx")
        s_rows = [sem("s_rows0"), sem("s_rows1")]
        s_unit = sem("s_unit")
        s_unit_act = sem("s_unit_act")
        s_lo = sem("s_lo")
        s_pairs = sem("s_pairs")
        s_l0 = sem("s_l0")
        s_x1hi = sem("s_x1hi")
        s_x1 = sem("s_x1")
        s_embs = sem("s_embs")
        s_embd = sem("s_embd")
        s_y = sem("s_y")
        s_scaled = sem("s_scaled")
        s_gadd = sem("s_gadd")
        s_chain = sem("s_chain")
        s_outer = sem("s_outer")
        s_outer_sb = sem("s_outer_sb")
        s_w2 = sem("s_w2")
        s_top = sem("s_top")
        s_w2hi = sem("s_w2hi")
        s_w2lo = sem("s_w2lo")
        s_ohi = sem("s_ohi")
        s_olo = sem("s_olo")
        s_l2 = sem("s_l2")
        s_z = sem("s_z")
        s_part = sem("s_part")
        s_h1ps = sem("s_h1ps")
        s_h1 = sem("s_h1")
        s_h2ps = sem("s_h2ps")
        s_h2 = sem("s_h2")
        s_yps = sem("s_yps")
        s_ysb = sem("s_ysb")
        s_out = sem("s_out")
        s_pe_passed = sem("s_pe_passed")
        s_pool_passed = sem("s_pool_passed")

        w2_raw = pairs_flat[:, 0:NF * H]
        wt1_sb = pairs_flat[:, NF * H:NF * H + 3 * T1].rearrange("p (c n) -> p c n", c=3)
        wt1c_sb = pairs_flat[0:CTX, NF * H + 3 * T1:NF * H + 4 * T1]
        wt2_sb = emb_t_flat[:, 0:4 * T2].rearrange("p (c n) -> p c n", c=4)
        ctx_sb = emb_t_flat[0:CTX, 4 * T2:4 * T2 + B]
        w1_raw = outer_flat[:, 0:NF * H]
        w0a_raw = outer_flat[:, NF * H:NF * H + NCH * H]
        w0b_raw = outer_flat[:, NF * H + NCH * H:NF * H + 2 * NCH * H]
        w0s = outer_flat[:, NF * H + 2 * NCH * H:NF * H + 3 * NCH * H]
        w0_hi_f = w0_hi[:, :, :].rearrange("p c h -> p (c h)")
        w0_lo_f = w0_lo[:, :, :].rearrange("p c h -> p (c h)")
        b0_c, b2_c, b0x, b2x = (bias[:, i:i + 1] for i in range(4))
        N_PAIRS_ALL = (NG + 1) * TG

        def chunk_rows(c):
            return min(P, NPAIR - c * P)

        def fields_of(k):
            return FIELDS4[k] * 4, min(4, NF - FIELDS4[k] * 4)

        def unit_number(g, u):
            return u if g is None else count(g, NU, NPU + u)

        def unit_bank(g, u):
            return scr[u % 2] if g is None else scr[(NPU + NU + u) % 2]

        def chunk_number(g, c):
            return c if g is None else count(g, NCH, NCH + c)

        def seq(g):
            return PRO_UNITS if g is None else UNITS

        def prev_unit(g, u):
            if u >= 2:
                return g, u - 2
            if g is None:
                return None
            if isinstance(g, int) and g == 0:
                return None, NPU - 2 + u
            return g - 1, NU - 2 + u

        def chunks_before(units, u):
            return sum(e[0] == "T" for e in units[:u])

        def w2j_hi(i):
            return w0_hi[:, i, :]

        def w2j_lo(i):
            return w0_lo[:, i, :]

        def oj_hi(i):
            return [pt_hi[:, 0, :], pt_hi[:, 1, :], x1_hi[:, 0, :]][i]

        def oj_lo(i):
            return [pt_lo[:, 0, :], pt_lo[:, 1, :], x1_lo[:, 0, :]][i]

        def rows_count(g, par):
            if isinstance(g, int):
                return 16 * QF * (g // 2 + 2)
            return g * (8 * QF) + (-par + 4) * (8 * QF)

        block = es.enter_context(nc.Block())

        @block.sync
        def _(sp):
            sp.dma_start(ids_sb[:, :], ids).then_inc(s_ids, 16)
            sp.dma_start(first_sb[:, :], first_row).then_inc(s_ids, 16)
            sp.dma_start(ident[:, :], ident_in).then_inc(s_const, 16)
            sp.dma_start(bmask[:, :], bmask_in).then_inc(s_const, 16)
            sp.dma_start(bias[:, 0:1], b0).then_inc(s_const, 16)
            sp.dma_start(bias[:, 1:2], b2).then_inc(s_const, 16)
            sp.dma_start(bias[:, 4:8], bt1).then_inc(s_const, 16)
            sp.dma_start(bias[:, 8:10], bt2).then_inc(s_const, 16)
            sp.dma_start(bias[:, 10:12], wt3).then_inc(s_const, 16)
            sp.dma_start(sg[1][:, 3 * H:4 * H], b1.broadcast_to((P, H))).then_inc(s_const, 16)
            sp.dma_start(w0a_raw, w0a).then_inc(s_w0, 16)
            sp.dma_start(w0b_raw, w0b).then_inc(s_w0, 16)
            sp.dma_start(w1_raw, w1).then_inc(s_w1, 16)
            sp.wait_ge(s_pairs, N_PAIRS_ALL)
            sp.wait_ge(s_unit, NPU + NU * (NG - 1))
            sp.dma_start(w2_raw, w2).then_inc(s_w2, 16)
            sp.dma_start(wt1_sb, wt1).then_inc(s_top, 16)
            sp.dma_start(wt1c_sb, wt1c).then_inc(s_top, 16)
            sp.dma_start(wt2_sb, wt2).then_inc(s_top, 16)
            sp.dma_start(ctx_sb, ctx_t).then_inc(s_top, 16)
            sp.wait_ge(s_ysb, 1)
            sp.dma_start(out, acc[0:1, 0:B]).then_inc(s_out, 16)
            sp.wait_ge(s_out, 16)

        @block.tensor
        def _(pe):
            def free_unit(g, u):
                before = prev_unit(g, u)
                if before is None:
                    return
                bg, bu = before
                if seq(bg)[bu][0] == "T":
                    pe.wait_ge(s_lo, chunk_number(bg, chunks_before(seq(bg), bu)) + 1)
                else:
                    pe.wait_ge(s_unit_act, unit_number(bg, bu) + 1)

            def step_e(g, u, k, par, rows_wait):
                free_unit(g, u)
                ps = unit_bank(g, u)
                if k == 0:
                    pe.wait_ge(s_rows[par], rows_wait)
                if k < 4:
                    for i in range(4):
                        last = nc.tensor.transpose(ps[0:QF, i * P:(i + 1) * P], rows[:, par, :, 4 * k + i],
                                                   ident[:, :])
                else:
                    pe.wait_ge(s_unit_act, unit_number(g, u - UNIT_BACK(g, u)) + 1)
                    pe.sem_inc(s_pe_passed)
                    for t in range(TG):
                        for q in range(4):
                            last = nc.tensor.transpose(
                                ps[:, t * NJ + q * QF:t * NJ + (q + 1) * QF],
                                emb_t[0:QF, q, t * TB:(t + 1) * TB, :].rearrange("p b d -> p (b d)"),
                                ident[0:QF, 0:QF])
                last.then_inc(s_unit, 1)

            def UNIT_BACK(g, u):
                return next(n for n in range(1, u + 1) if seq(g)[u - n] == ("E", 3))

            def step_t(g, u, c, par, pairs_wait):
                free_unit(g, u)
                ps = unit_bank(g, u)
                if c == 0:
                    pe.wait_ge(s_pairs, pairs_wait)
                n = chunk_rows(c)
                for t in range(TG):
                    last = nc.tensor.transpose(ps[0:n, t * P:(t + 1) * P], pairs[:, par, t, c * P:c * P + n],
                                               ident[:, :])
                last.then_inc(s_unit, 1)

            def step_m(g, c, x1_free):
                pe.wait_ge(s_lo, chunk_number(g, c) + 1)
                if c == 0 and x1_free is not None:
                    pe.wait_ge(s_x1, x1_free)
                n, r = chunk_rows(c), c % 2
                nc.tensor.matmul(ps_x1[:, :], w0_hi[0:n, c, :], pt_hi[0:n, r, :], start=(c == 0), stop=False)
                nc.tensor.matmul(ps_x1[:, :], w0_lo[0:n, c, :], pt_hi[0:n, r, :], start=False, stop=False)
                nc.tensor.matmul(ps_x1[:, :], w0_hi[0:n, c, :], pt_lo[0:n, r, :], start=False,
                                 stop=(c == NCH - 1)).then_inc(s_l0, 1)

            def outer_products(g, t):
                n = count(g, TG, t)
                pe.wait_ge(s_chain, count(g, TG * CHAIN, (t + 1) * CHAIN))
                pe.wait_ge(s_embd, n + 1)
                if not (isinstance(n, int) and n == 0):
                    pe.wait_ge(s_outer_sb, n)
                nc.tensor.matmul(ps_g[:, 0:TB * NJ], x2[:, t % 2, :],
                                 embd[:, :, :].rearrange("p b j -> p (b j)"),
                                 start=True, stop=True).then_inc(s_outer, 1)

            def body(g, par, first=False, last=False):
                for s in range(NS):
                    t, k = divmod(s, NBK)
                    for what, i in PE_EXTRA.get(s, []):
                        u = UNITS.index((what, i)) if what != "M" else None
                        if last:
                            continue
                        if what == "T":
                            step_t(g, u, i, 1 - par, count(g, TG, 2 * TG))
                        elif what == "E":
                            step_e(g, u, i, par, rows_count(g, par))
                        else:
                            step_m(g, i, count(g, 2, 2))
                    if k == G_SLOT and (t or not first):
                        outer_products(g if t else g - 1, (t - 1) % TG)
                    if s == 0:
                        pe.wait_ge(s_x1, count(g, 2, 1))
                    if not (first and s < YB):
                        tb, kb = divmod((s - YB) % NS, NBK)
                        gb = g if s >= YB else g - 1
                        if KIND[kb] == "D":
                            pe.wait_ge(s_chain, count(gb, TG * CHAIN, tb * CHAIN + DONE[kb]))
                        else:
                            n = sum(KIND[i] != "D" for i in range(kb + 1))
                            pe.wait_ge(s_scaled, count(gb, TG * N_ACT, tb * N_ACT + n))
                    f, m = fields_of(k)
                    o = y[s % YB][:, 0:m * H]
                    if first and t == 0:
                        pe.wait_ge(s_w1lo, FIELDS4[k] + 1)
                    hi = x1_hi[:, par, t * P:(t + 1) * P]
                    lo = x1_lo[:, par, t * P:(t + 1) * P]
                    nc.tensor.matmul(o, hi, w_hi[:, f * H:(f + m) * H], start=True, stop=False)
                    nc.tensor.matmul(o, hi, w_lo[:, f * H:(f + m) * H], start=False, stop=False)
                    nc.tensor.matmul(o, lo, w_hi[:, f * H:(f + m) * H], start=False, stop=True).then_inc(s_y, 1)

            pe.wait_ge(s_const, 8 * 16)
            for u, (what, i) in enumerate(PRO_UNITS):
                if what == "E":
                    n = u // 5
                    step_e(None, u, i, n, 16 * QF)
                else:
                    if i == 0:
                        pe.wait_ge(s_w0lo, 1)
                    step_t(None, u, i, 0, TG)
                    if i:
                        step_m(None, i - 1, None)
            step_m(None, NCH - 1, None)
            body(0, 0, first=True)
            with pe.Fori(0, NG // 2 - 1) as pair:
                body(pair * 2 + 1, 1)
                body(pair * 2 + 2, 0)
            body(NG - 1, 1, last=True)
            outer_products(NG - 1, TG - 1)

            pe.wait_ge(s_top, 4 * 16)
            pe.wait_ge(s_outer_sb, NG * TG)
            pe.wait_ge(s_z, 1)
            for m in range(4):
                o, c = y[m][:, :], slice(m * P, (m + 1) * P)
                nc.tensor.matmul(o, wt1_sb[:, 0, c], scaled[:, 4, :], start=True, stop=False)
                nc.tensor.matmul(o, wt1_sb[:, 1, c], outer[:, NF, :], start=False, stop=False)
                nc.tensor.matmul(o, wt1c_sb[:, c], ctx_sb, start=False, stop=False).then_inc(s_part, 1)
            def fields3(j, start=False, stop=False):
                for i in range(3):
                    pe.wait_ge(s_w2lo, j + (i + 1))
                    pe.wait_ge(s_olo, j + (i + 1))
                    nc.tensor.matmul(ps_x1[:, :], w2j_hi(i), oj_hi(i), start=start and i == 0, stop=False)
                    nc.tensor.matmul(ps_x1[:, :], w2j_lo(i), oj_hi(i), start=False, stop=False)
                    nc.tensor.matmul(ps_x1[:, :], w2j_hi(i), oj_lo(i), start=False,
                                     stop=stop and i == 2).then_inc(s_l2, 1)

            fields3(0, start=True)
            with pe.Fori(1, NF // 3 - 1) as three:
                fields3(three * 3)
            fields3(NF - 3, stop=True)
            pe.wait_ge(s_z, 2)
            for m in range(4):
                nc.tensor.matmul(y[m][:, :], wt1_sb[:, 2, m * P:(m + 1) * P], scaled[:, 5, :], start=False,
                                 stop=True).then_inc(s_h1ps, 1)
            for m in range(2):
                for c in range(4):
                    pe.wait_ge(s_h1, c + 1)
                    last = nc.tensor.matmul(scr[m][:, :], wt2_sb[:, c, m * P:(m + 1) * P], scaled[:, c, :],
                                            start=(c == 0), stop=(c == 3))
                last.then_inc(s_h2ps, 1)
            for c in range(2):
                pe.wait_ge(s_h2, c + 1)
                last = nc.tensor.matmul(ps_g[0:1, :], bias[:, 10 + c:11 + c], scaled[:, 6 + c, :],
                                        start=(c == 0), stop=(c == 1))
            last.then_inc(s_yps, 1)

        @block.scalar
        def _(act):
            def unit(g, u, what, i, par):
                act.wait_ge(s_unit, unit_number(g, u) + 1)
                ps = unit_bank(g, u)
                if what == "T":
                    n = chunk_number(g, i)
                    if not (isinstance(n, int) and n < 2):
                        act.wait_ge(s_l0, n - (1 if i >= 2 else i))
                    r = chunk_rows(i)
                    nc.scalar.copy(pt_hi[0:r, i % 2, :], ps[0:r, :]).then_inc(s_unit_act, 1)
                elif i < 4:
                    nc.scalar.copy(
                        emb_t[0:QF, :, :, 4 * i:4 * i + 4].rearrange("p q b d -> p d (q b)"),
                        ps[0:QF, :].rearrange("p (d n) -> p d n", d=4)).then_inc(s_unit_act, 1)
                else:
                    if g is not None:
                        act.wait_ge(s_embs, count(g, 1, 1))
                    nc.scalar.copy(emb[:, par, :, :].rearrange("p t j -> p (t j)"),
                                   ps[:, 0:TG * NJ]).then_inc(s_unit_act, 1)

            def x1_high(g, par, chunks, y_before):
                act.wait_ge(s_l0, chunks)
                if y_before is not None:
                    act.wait_ge(s_y, y_before)
                nc.scalar.activation(x1_hi[:, par, :], ps_x1[:, :], ACT.Identity, bias=b0_c,
                                     scale=1.0).then_inc(s_x1hi, 1)

            def outer_out(g, t):
                n = count(g, TG, t)
                act.wait_ge(s_outer, n + 1)
                nc.scalar.copy(outer[:, :, bass.ds(n * TB, TB)],
                               ps_g[:, 0:TB * NJ].rearrange("p (b j) -> p j b", b=TB)).then_inc(s_outer_sb, 1)

            def body(g, par, first=False, last=False):
                for s in range(NS):
                    t, k = divmod(s, NBK)
                    for what, i in ACT_EXTRA.get(s, []):
                        if not last:
                            unit(g, UNITS.index((what, i)), what, i, par)
                    if s == X1_ACT and not last:
                        x1_high(g, 1 - par, count(g, NCH, 2 * NCH), count(g, NS, 0) if not first else None)
                    if k == G_ACT and (t or not first):
                        outer_out(g if t else g - 1, (t - 1) % TG)
                    if KIND[k] == "D":
                        continue
                    if s == 0:
                        act.wait_ge(s_embs, count(g, 1, 1))
                    act.wait_ge(s_y, count(g, NS, s + 1))
                    f, m = fields_of(k)
                    fresh = first and t == 0
                    if KIND[k] == "V":
                        v = V_SLOTS.index(k)
                        dst = sv[v]
                        if not fresh:
                            after = DONE[D_SLOTS[0]] if v == 0 else DONE["V"]
                            act.wait_ge(s_chain, count(g, TG * CHAIN, (t - 1) * CHAIN + after))
                    else:
                        v = G_SLOTS.index(k)
                        dst = sg[v]
                        if not fresh:
                            act.wait_ge(s_gadd, count(g, TG * 2, (t - 1) * 2 + (1 if v < 2 else 2)))
                    for i in range(m):
                        last_i = nc.scalar.mul(dst[:, i * H:(i + 1) * H], y[s % YB][:, i * H:(i + 1) * H],
                                               embs[:, par, t, f + i:f + i + 1])
                    last_i.then_inc(s_scaled, 1)

            act.wait_ge(s_const, 8 * 16)
            nc.scalar.mul(bias[:, 2:4], bias[:, 0:2], float(D))
            act.wait_ge(s_w0sum, 1)
            nc.scalar.copy(w0_hi_f, w0s).then_inc(s_w0hi, 1)
            act.wait_ge(s_w1, 16)
            for n in range(NBK):
                c = slice(n * 512, min((n + 1) * 512, NF * H))
                nc.scalar.copy(w_hi[:, c], w1_raw[:, c]).then_inc(s_w1hi, 1)
            for u, (what, i) in enumerate(PRO_UNITS):
                unit(None, u, what, i, u // 5 if what == "E" else 0)
            x1_high(None, 0, NCH, None)
            body(0, 0, first=True)
            with act.Fori(0, NG // 2 - 1) as pair:
                body(pair * 2 + 1, 1)
                body(pair * 2 + 2, 0)
            body(NG - 1, 1, last=True)
            outer_out(NG - 1, TG - 1)

            act.wait_ge(s_x1, 2 * NG)
            act.wait_ge(s_gadd, 2 * NG * TG)
            nc.scalar.activation(scaled[:, 4, :], z0[:, :], ACT.Identity, bias=b0x, scale=1.0).then_inc(s_z, 1)
            def high3(j, first=False):
                for i in range(3):
                    if not first:
                        act.wait_ge(s_l2, j + (i - 2))
                    nc.scalar.copy(oj_hi(i), outer_flat[:, bass.ds((j + i) * B, B)]).then_inc(s_ohi, 1)

            act.wait_ge(s_outer_sb, NG * TG)
            act.wait_ge(s_l0, NCH * NG)
            act.wait_ge(s_y, NS * NG)
            high3(0, first=True)
            with act.Fori(1, NF // 3) as three:
                high3(three * 3)
            act.wait_ge(s_l2, NF)
            nc.scalar.activation(scaled[:, 5, :], ps_x1[:, :], ACT.Identity, bias=b2x, scale=1.0).then_inc(s_z, 1)
            for m in range(4):
                act.wait_ge(s_h1ps, m + 1)
                nc.scalar.activation(scaled[:, m, :], y[m][:, :], ACT.Relu, bias=bias[:, 4 + m:5 + m],
                                     scale=1.0).then_inc(s_h1, 1)
            for m in range(2):
                act.wait_ge(s_h2ps, m + 1)
                nc.scalar.activation(scaled[:, 6 + m, :], scr[m][:, :], ACT.Relu, bias=bias[:, 8 + m:9 + m],
                                     scale=1.0).then_inc(s_h2, 1)
            act.wait_ge(s_yps, 1)
            nc.scalar.copy(acc[0:1, 0:B], ps_g[0:1, :]).then_inc(s_ysb, 1)

        def tile_pairs(eng, par, t):
            at = 0
            for a, m in FBLOCKS:
                n = NF - a
                last = eng.tensor_tensor(
                    pairs[:, par, t, at:at + m * n].rearrange("p (j k) -> p j k", j=m),
                    emb[:, par, t, a:a + m].unsqueeze(2).broadcast_to((P, m, n)),
                    emb[:, par, t, a:NF].unsqueeze(1).broadcast_to((P, m, n)), ALU.mult)
                at += m * n
            return last

        @block.vector
        def _(dve):
            def chunk_low(g, c, u):
                dve.wait_ge(s_unit_act, unit_number(g, u) + 1)
                r = chunk_rows(c)
                nc.vector.tensor_tensor(pt_lo[0:r, c % 2, :], unit_bank(g, u)[0:r, :],
                                        pt_hi[0:r, c % 2, :].bitcast(F32), ALU.subtract).then_inc(s_lo, 1)

            def x1_low(g1, par):
                dve.wait_ge(s_x1hi, count(g1, 1, 1))
                nc.vector.scalar_tensor_tensor(out=x1_lo[:, par, :], in0=ps_x1[:, :], scalar=b0_c,
                                               in1=x1_hi[:, par, :].bitcast(F32), op0=ALU.add,
                                               op1=ALU.subtract).then_inc(s_x1, 1)
                nc.vector.reduce_sum(z0[:, bass.ds(g1 * GB, GB)],
                                     ps_x1[:, :].rearrange("p (b d) -> p b d", d=D),
                                     axis=AX.X).then_inc(s_x1, 1)

            def body(g, par, first=False, last=False):
                for s in range(NS):
                    t, k = divmod(s, NBK)
                    base = t * CHAIN

                    def chained(n):
                        v = count(g, TG * CHAIN, base + n)
                        if not (isinstance(v, int) and v <= 0):
                            dve.wait_ge(s_chain, v)

                    for what, i in DVE_EXTRA.get(s, []):
                        if not last:
                            chunk_low(g, i, UNITS.index((what, i)))
                    if s == X1_DVE and not last:
                        x1_low(g + 1, 1 - par)
                    if s == 0:
                        dve.wait_ge(s_embs, count(g, 1, 1))
                    for step in [w for w, at in STEPS if at == k]:
                        if step in D_SLOTS:
                            f, m = fields_of(step)
                            bank = y[(t * NBK + step) % YB]
                            dve.wait_ge(s_y, count(g, NS, t * NBK + step + 1))
                            start = step == D_SLOTS[0]
                            if start:
                                a = sum(KIND[i] != "D" for i in range(V_SLOTS[0] + 1))
                                dve.wait_ge(s_scaled, count(g, TG * N_ACT, t * N_ACT + a))
                            for i in range(m):
                                b = slice(i * H, (i + 1) * H)
                                if start and i == 0:
                                    chained(DONE["F"] - CHAIN)
                                elif not start:
                                    chained(DONE[D_SLOTS[D_SLOTS.index(step) - 1]] - 4 + i + 1)
                                nc.vector.scalar_tensor_tensor(
                                    out=acc[:, b], in0=bank[:, b], scalar=embs[:, par, t, f + i:f + i + 1],
                                    in1=sv[0][:, b] if start else acc[:, b],
                                    op0=ALU.mult, op1=ALU.add).then_inc(s_chain, 1)
                        elif step == "V":
                            a = sum(KIND[i] != "D" for i in range(V_SLOTS[2] + 1))
                            dve.wait_ge(s_scaled, count(g, TG * N_ACT, t * N_ACT + a))
                            chained(0)
                            nc.vector.tensor_tensor(acc_b[:, :], sv[1], sv[2], ALU.add).then_inc(s_chain, 1)
                        elif step == "G":
                            dve.wait_ge(s_gadd, count(g, TG * 2, t * 2 + 2))
                            chained(DONE["V"])
                            nc.vector.tensor_tensor(acc_b[:, :], acc_b[:, :], gsum[1],
                                                    ALU.add).then_inc(s_chain, 1)
                        elif step == "A":
                            chained(DONE["G"])
                            nc.vector.tensor_tensor(acc[:, :], acc[:, :], acc_b[:, :],
                                                    ALU.add).then_inc(s_chain, 1)
                        elif step == "F":
                            chained(DONE["A"])
                            nc.vector.tensor_tensor(acc_b[:, 0:256], acc[:, 0:256], acc[:, 256:512],
                                                    ALU.add).then_inc(s_chain, 1)
                        else:
                            chained(DONE["F"])
                            tile_before = count(g, TG, t - 1)
                            if not (isinstance(tile_before, int) and tile_before <= 0):
                                dve.wait_ge(s_outer, tile_before)
                            nc.vector.tensor_tensor(x2[:, t % 2, :], acc_b[:, 0:H], acc_b[:, H:2 * H],
                                                    ALU.add).then_inc(s_chain, 1)

            dve.wait_ge(s_w0, 32)
            nc.vector.tensor_tensor(w0s, w0a_raw, w0b_raw, ALU.add).then_inc(s_w0sum, 1)
            dve.wait_ge(s_w0hi, 1)
            nc.vector.tensor_tensor(w0_lo_f, w0s, w0_hi_f.bitcast(F32), ALU.subtract).then_inc(s_w0lo, 1)
            for n in range(NBK):
                dve.wait_ge(s_w1hi, n + 1)
                c = slice(n * 512, min((n + 1) * 512, NF * H))
                nc.vector.tensor_tensor(w_lo[:, c], w1_raw[:, c], w_hi[:, c].bitcast(F32),
                                        ALU.subtract).then_inc(s_w1lo, 1)
            for g0 in range(2):
                dve.wait_ge(s_unit_act, 5 * (g0 + 1))
                for t in range(TG):
                    tile_pairs(nc.vector, g0, t).then_inc(s_pairs, 1)
            for c in range(NCH):
                chunk_low(None, c, 10 + c)
            x1_low(0, 0)
            body(0, 0, first=True)
            with dve.Fori(0, NG // 2 - 1) as pair:
                body(pair * 2 + 1, 1)
                body(pair * 2 + 2, 0)
            body(NG - 1, 1, last=True)
            with dve.Fori(0, NF // 3) as three:
                j = three * 3
                for i in range(3):
                    dve.wait_ge(s_ohi, j + (i + 1))
                    nc.vector.tensor_tensor(oj_lo(i), outer_flat[:, bass.ds((j + i) * B, B)],
                                            oj_hi(i).bitcast(F32), ALU.subtract).then_inc(s_olo, 1)

        @block.gpsimd
        def _(pool):
            def row_numbers(g3, par):
                pool.sem_inc(s_pool_passed)
                nc.gpsimd.tensor_tensor(idx[:, par, :], ids_sb[:, bass.ds(g3 * QF, QF)], first_sb[:, :],
                                        ALU.add).then_inc(s_idx, 1)

            def gather(par, i):
                nc.gpsimd.indirect_dma_start(
                    out=rows[:, par, i, :], out_offset=None, in_=table,
                    in_offset=bass.IndirectOffsetOnAxis(ap=idx[:, par, i:i + 1], axis=0)).then_inc(s_rows[par], 16)

            def copy_embs(par):
                pool.sem_inc(s_pool_passed)
                nc.gpsimd.tensor_copy(embs[:, par, :, 0:NF], emb[:, par, :, 0:NF]).then_inc(s_embs, 1)

            def block_diagonal(g, par, t):
                n = count(g, TG, t)
                if not (isinstance(n, int) and n < 1):
                    pool.wait_ge(s_outer, n)
                nc.gpsimd.tensor_tensor(embd[:, :, :],
                                        embs[:, par, t, :].unsqueeze(1).broadcast_to((P, TB, NJ)),
                                        bmask[:, :].unsqueeze(2).broadcast_to((P, TB, NJ)),
                                        ALU.mult).then_inc(s_embd, 1)

            def add(g, t, which, first):
                slot = G_SLOTS[which + 1]
                a = sum(KIND[i] != "D" for i in range(slot + 1))
                pool.wait_ge(s_scaled, count(g, TG * N_ACT, t * N_ACT + a))
                if which == 0:
                    if not (first and t == 0):
                        pool.wait_ge(s_gadd, count(g, TG * 2, t * 2))
                    nc.gpsimd.tensor_tensor(gsum[0], sg[0], sg[1], ALU.add).then_inc(s_gadd, 1)
                else:
                    pool.wait_ge(s_gadd, count(g, TG * 2, t * 2 + 1))
                    if not (first and t == 0):
                        pool.wait_ge(s_chain, count(g, TG * CHAIN, (t - 1) * CHAIN + DONE["G"]))
                    nc.gpsimd.tensor_tensor(gsum[1], gsum[0], sg[2], ALU.add).then_inc(s_gadd, 1)

            def body(g, par, first=False, last=False):
                pool.wait_ge(s_embs, count(g, 1, 1))
                for (what, i), _ in sorted(POOL_AT.items(), key=lambda x: x[1]):
                    if what == "diagonal":
                        block_diagonal(g, par, i)
                    elif what == "add":
                        add(g, i // 2, i % 2, first)
                    elif last:
                        continue
                    elif what == "copy":
                        if first:
                            pool.wait_ge(s_unit_act, 10)
                        else:
                            pool.wait_ge(s_scaled, count(g, TG * N_ACT, 0))
                            pool.wait_ge(s_chain, count(g, TG * CHAIN, DONE["A"] - CHAIN))
                        copy_embs(1 - par)
                    elif what == "gather":
                        if i == 0:
                            pool.wait_ge(s_unit, 9 if first else unit_number(g - 1, UNITS.index(("E", 3))) + 1)
                            row_numbers(g + 3, 1 - par)
                            pool.wait_ge(s_idx, count(g, 1, 4))
                            pool.sem_inc(s_pool_passed)
                        gather(1 - par, i)
                    else:
                        if i == 0:
                            pool.wait_ge(s_unit_act, unit_number(g, UNITS.index(("E", 4))) + 1)
                            pool.wait_ge(s_unit, NPU if first else unit_number(g - 1, UNITS.index(("T", 6))) + 1)
                        tile_pairs(nc.gpsimd, par, i).then_inc(s_pairs, 1)

            nc.gpsimd.memset(embs[:, :, :, NF:NJ], 1.0).then_inc(s_ones, 1)
            pool.wait_ge(s_ids, 32)
            for g0 in range(3):
                if g0 == 2:
                    pool.wait_ge(s_unit, 4)
                row_numbers(g0, g0 % 2)
                pool.wait_ge(s_idx, g0 + 1)
                for i in range(QF):
                    gather(g0 % 2, i)
                if g0 == 1:
                    pool.wait_ge(s_ones, 1)
                    pool.wait_ge(s_const, 8 * 16)
                    pool.wait_ge(s_unit_act, 5)
                    copy_embs(0)
            body(0, 0, first=True)
            with pool.Fori(0, NG // 2 - 1) as pair:
                body(pair * 2 + 1, 1)
                body(pair * 2 + 2, 0)
            body(NG - 1, 1, last=True)
            pool.wait_ge(s_rows[0], 16 * QF * (NIDX // 2))
            pool.wait_ge(s_rows[1], 16 * QF * (NIDX // 2))
            pool.wait_ge(s_w2, 16)
            pool.wait_ge(s_l0, NCH * NG)

            def weights3(j, first=False):
                for i in range(3):
                    if not first:
                        pool.wait_ge(s_l2, j + (i - 2))
                    pool.sem_inc(s_pool_passed)
                    nc.gpsimd.tensor_copy(w2j_hi(i), w2_raw[:, bass.ds((j + i) * H, H)]).then_inc(s_w2hi, 1)
                    pool.wait_ge(s_w2hi, j + (i + 1))
                    pool.sem_inc(s_pool_passed)
                    nc.gpsimd.tensor_tensor(w2j_lo(i), w2_raw[:, bass.ds((j + i) * H, H)],
                                            w2j_hi(i).bitcast(F32), ALU.subtract).then_inc(s_w2lo, 1)

            weights3(0, first=True)
            with pool.Fori(1, NF // 3) as three:
                weights3(three * 3)


def _layout(inputs):
    a = {k: np.asarray(v) for k, v in inputs.items()}
    table = np.concatenate([a[f"tbl_{f}"] for f in range(NF)], axis=0)
    ids = np.zeros((NIDX * GB, NJ), a["ids"].dtype)
    ids[0:B, 0:NF] = a["ids"]
    ids = ids.reshape(NIDX, GB, 4, QF).transpose(2, 1, 0, 3).reshape(P, NIDX * QF)
    first = np.zeros(NJ, np.int32)
    first[0:NF] = np.cumsum([0] + VOCAB[:-1])
    first_row = np.repeat(first.reshape(4, 1, QF), GB, axis=1).reshape(P, QF)
    ident = np.eye(P, dtype=np.float32)
    bmask = np.repeat(np.eye(TB, dtype=np.float32), D, axis=0)
    w0 = a["L0_rec_W0"].reshape(H, NF, NF)
    w0a = np.zeros((NCH * P, H), w0.dtype)
    w0b = np.zeros((NCH * P, H), w0.dtype)
    at = 0
    for f, m in FBLOCKS:
        n = NF - f
        w0a[at:at + m * n] = w0[:, f:f + m, f:].reshape(H, m * n).T
        other = w0[:, f:, f:f + m].transpose(2, 1, 0).copy()
        other[:, 0:m] = 0
        w0b[at:at + m * n] = other.reshape(m * n, H)
        at += m * n

    def chunks(x, n):
        return x.reshape(n, P, -1).transpose(1, 0, 2)

    def by_field(w):
        return w.reshape(H, NF, H).transpose(2, 1, 0).reshape(H, NF * H)

    return [
        ("table", table), ("ids_g", ids), ("first_row", first_row), ("ident_c", ident), ("bmask_c", bmask),
        ("w0a", chunks(w0a, NCH).reshape(P, NCH * H)), ("w0b", chunks(w0b, NCH).reshape(P, NCH * H)),
        ("w1", by_field(a["L0_rec_W1"])), ("w2", by_field(a["L0_rec_W2"])),
        ("b0", a["L0_rec_b0"].reshape(P, 1)), ("b1", a["L0_rec_b1"].reshape(1, H)),
        ("b2", a["L0_rec_b2"].reshape(P, 1)),
        ("wt1", chunks(a["W_top1"][0:3 * H], 3)), ("wt1c", a["W_top1"][3 * H:]),
        ("bt1", a["b_top1"].reshape(4, P).T), ("wt2", chunks(a["W_top2"], 4)),
        ("bt2", a["b_top2"].reshape(2, P).T), ("wt3", a["W_top3"].reshape(2, P).T),
        ("ctx_t", a["dense_ctx"].T),
    ]


def kernel(**inputs):
    import concourse.bacc as bacc
    from concourse.bass_utils import run_bass_kernel_spmd

    nc = bacc.Bacc("TRN2", target_bir_lowering=False, num_devices=1)
    arrays, args = {}, []
    for name, a in _layout(inputs):
        a = np.ascontiguousarray(a)
        arrays[f"in_{name}"] = a
        args.append(nc.dram_tensor(f"in_{name}", a.shape, mybir.dt.from_np(a.dtype), kind="ExternalInput").ap())
    res = nc.dram_tensor("out_0", (1, B), F32, kind="ExternalOutput").ap()
    build(nc, *args, res)
    r = run_bass_kernel_spmd(nc, [arrays], core_ids=[0])
    return r.results[0]["out_0"].reshape(B, 1)
```

```python
import concourse.bass as bass
from concourse import mybir
from contextlib import ExitStack
import numpy as np

F32 = mybir.dt.float32
F32R = mybir.dt.float32r
I32 = mybir.dt.int32
ALU = mybir.AluOpType
ACT = mybir.ActivationFunctionType
AX = mybir.AxisListType

VOCAB = [1250, 1250, 1000, 12500, 125000, 1250, 1000, 12500, 12500, 125000, 125000, 125000, 12500,
         125000, 1250, 1250, 1000, 125000, 1000, 1250, 12500, 125000, 1000, 125000, 1000, 12500, 1000,
         1000, 12500, 1250, 1250, 125000, 1000, 1000, 1250, 1250, 1000, 1250, 1250]
B, NF, D, H = 512, 39, 16, 128
CTX = 16
T1, T2 = 512, 256
P = 128

TB = P // D
TG = 4
GB = TB * TG
NG = B // GB
NJ = 40
PG = 2
GB2 = PG * GB
QF = NJ // 2
HALF1 = 32
NCH = 7
FBLOCKS = [(0, 7), (7, 7), (14, 7), (21, 6), (27, 6), (33, 6)]
BLOCK_PAIRS = [m * (NF - a) for a, m in FBLOCKS]
BLOCK_ENDS = [sum(BLOCK_PAIRS[:i + 1]) for i in range(len(FBLOCKS))]
NPAIR = BLOCK_ENDS[-1]
assert (NCH - 1) * P < NPAIR <= NCH * P
NBK = 10
NS = TG * NBK
YB = 4

KIND = "GGVGVDDDVD"
FIELDS4 = [2, 9, 3, 1, 0, 4, 5, 6, 7, 8]
LAST4 = FIELDS4.index(9)
D_SLOTS, V_SLOTS, G_SLOTS = ([k for k in range(NBK) if KIND[k] == x] for x in "DVG")
assert len(V_SLOTS) == 3 and len(G_SLOTS) == 3 and LAST4 in G_SLOTS[0:2]
N_ACT = len(V_SLOTS) + len(G_SLOTS)
STEPS = [(5, 5), (6, 6), (7, 7), (9, 9), ('V', 9), ('G', 9), ('A', 9), ('F', 9), ('H', 9)]
DONE, n = {}, 0
for what, _ in STEPS:
    n += 4 if what in D_SLOTS else 1
    DONE[what] = n
CHAIN = n

PE_AT = {("T", 0): 4, ("T", 1): 7, ("T", 2): 10, ("T", 3): 18, ("T", 4): 24, ("T", 5): 26, ("T", 6): 28, ("E", 0): 0, ("E", 1): 2, ("E", 2): 4, ("E", 3): 9, ("E", 4): 12, ("M", 0): 9, ("M", 1): 13, ("M", 2): 20, ("M", 3): 25, ("M", 4): 28, ("M", 5): 33, ("M", 6): 33}
E4_ODD = 1
ACT_LEAD = 1
DVE_LAG = 1
X1_ACT, X1_DVE = 33, 30


N_EVEN = 7
POOL_BOTH = {("copy", 0): 2.2}
POOL_BOTH |= {("diagonal", t): t * NBK + [8.1, 6.1, 8.1, 8.1][t] for t in range(TG)}
POOL_BOTH |= {("add", 2 * t + w): t * NBK + [4.5, 5.5][w] for t in range(TG) for w in range(2)}
GATHER_EVEN = [12, 15, 17, 17, 20, 28, 30]
GATHER_ODD = [0, 0, 4, 5, 10, 13, 15, 16, 19, 22, 25, 25, 30]
PAIRS_EVEN, PAIRS_ODD = [21, 21.9, 24, 30], [7, 15, 35, 38]
POOL_AT = [POOL_BOTH | {("gather", i): GATHER_EVEN[i] for i in range(N_EVEN)}
           | {("pairs", t): PAIRS_EVEN[t] for t in range(TG)},
           POOL_BOTH | {("gather", N_EVEN + i): GATHER_ODD[i] for i in range(QF - N_EVEN)}
           | {("pairs", t): PAIRS_ODD[t] for t in range(TG)}]


def extras(shift=0, kinds="TEM"):
    at = {}
    for (what, i), s in sorted(PE_AT.items(), key=lambda x: x[1]):
        if what in kinds:
            at.setdefault(max(0, s + shift), []).append((what, i))
    return at


def with_extras(shift, kinds):
    even = extras(shift, kinds)
    odd = {s: [e for e in es if e[0] != "E"] for s, es in even.items()}
    if "E" in kinds:
        odd.setdefault(max(0, E4_ODD + shift), []).insert(0, ("E", 4))
    return [even, odd]


PE_EXTRA, ACT_EXTRA, DVE_EXTRA = with_extras(0, "TEM"), with_extras(-ACT_LEAD, "TE"), with_extras(DVE_LAG, "T")
G_ACT = 8
G_SLOT = 7
UNITS = [[e for s in range(NS) for e in extra.get(s, []) if e[0] in "TE"] for extra in PE_EXTRA]
NU = [len(units) for units in UNITS]
assert NU[0] % 2 == 0 and NU[1] % 2 == 0
PRO = [("E", k, 0) for k in range(5)] + [("T", 0, 0), ("T", 1, 0), ("E", 4, 1)]
PRO += [("T", c, 0) for c in range(2, NCH)]
PRO_UNITS = [(what, i) for what, i, _ in PRO]
NPU = len(PRO_UNITS)                       
NIDX = NG + 2 * PG
COPY0_AT = 8


def count(g, per_group, within):
    return g * per_group + within


def build(nc, table, ids, first_row, ident_in, bmask_in, w0a, w0b, w1, w2, b0, b1, b2,
          wt1, wt1c, bt1, wt2, bt2, wt3, ctx_t, out):
    es = ExitStack()
    with es:
        def sb(name, shape, dt=F32):
            return es.enter_context(nc.sbuf_tensor(name, shape, dt))

        def pb(name):
            return es.enter_context(nc.psum_tensor(name, [P, 512], F32))

        def sem(name):
            return es.enter_context(nc.semaphore(name))

        w_hi = sb("w_hi", [P, NF * H], F32R)
        w_lo = sb("w_lo", [P, NF * H], F32R)
        w0_hi = sb("w0_hi", [P, NCH, H], F32R)
        w0_lo = sb("w0_lo", [P, NCH, H], F32R)
        outer = sb("outer", [P, NJ, B])
        outer_flat = outer[:, :, :].rearrange("p j b -> p (j b)")
        pairs = sb("pairs", [P, 2, TG, NPAIR])
        pairs_flat = pairs[:, :, :, :].rearrange("p a t n -> p (a t n)")
        pt_hi = sb("pt_hi", [P, 2, 512], F32R)
        pt_lo = sb("pt_lo", [P, 2, 512], F32R)
        x1_hi = sb("x1_hi", [P, 2, 512], F32R)
        x1_lo = sb("x1_lo", [P, 2, 512], F32R)
        scaled = sb("scaled", [P, 8, 512])
        sv = [scaled[:, i, :] for i in range(3)]
        sg = [scaled[:, 3 + i, :] for i in range(3)]
        gsum = [scaled[:, 6 + i, :] for i in range(2)]
        acc = sb("acc", [P, 512])
        acc_b = sb("acc_b", [P, 512])
        x2 = sb("x2", [P, 2, H])
        rows = [sb("rows", [P, QF, D]), sb("rows_second", [P, QF, D])]
        emb_t = sb("emb_t", [P, GB2, D])
        emb_t_flat = emb_t[:, :, :].rearrange("p b d -> p (b d)")
        ctx_all = sb("ctx_all", [P, B])
        emb = sb("emb", [P, 2, TG, NJ])
        embs = sb("embs", [P, 2, TG, NJ])
        embd = sb("embd", [P, TB, NJ])
        ids_sb = sb("ids_sb", [P, NIDX // PG * QF], I32)
        first_sb = sb("first_sb", [P, QF], I32)
        idx = sb("idx", [P, 2, QF], I32)
        ident = sb("ident", [P, P])
        bmask = sb("bmask", [P, TB])
        z0 = sb("z0", [P, B])
        bias = sb("bias", [P, 16])

        y = [pb(f"y{i}") for i in range(YB)]
        scr = [pb(f"scr{i}") for i in range(2)]
        ps_x1 = pb("ps_x1")
        ps_g = pb("ps_g")

        s_ids = sem("s_ids")
        s_const = sem("s_const")
        s_w0 = sem("s_w0")
        s_w1 = sem("s_w1")
        s_w0sum = sem("s_w0sum")
        s_w0hi = sem("s_w0hi")
        s_w0lo = sem("s_w0lo")
        s_w1hi = sem("s_w1hi")
        s_w1lo = sem("s_w1lo")
        s_ones = sem("s_ones")
        s_idx = sem("s_idx")
        s_rows = [sem("s_rows"), sem("s_rows_second")]
        s_zero = sem("s_zero")
        s_unit = sem("s_unit")
        s_unit_act = sem("s_unit_act")
        s_lo = sem("s_lo")
        s_pairs = sem("s_pairs")
        s_block = sem("s_block")
        s_l0 = sem("s_l0")
        s_x1hi = sem("s_x1hi")
        s_x1 = sem("s_x1")
        s_embs = sem("s_embs")
        s_embd = sem("s_embd")
        s_y = sem("s_y")
        s_scaled = sem("s_scaled")
        s_gadd = sem("s_gadd")
        s_chain = sem("s_chain")
        s_outer = sem("s_outer")
        s_outer_sb = sem("s_outer_sb")
        s_w2 = sem("s_w2")
        s_top = sem("s_top")
        s_w2hi = sem("s_w2hi")
        s_w2lo = sem("s_w2lo")
        s_ohi = sem("s_ohi")
        s_olo = sem("s_olo")
        s_l2 = sem("s_l2")
        s_z = sem("s_z")
        s_h1ps = sem("s_h1ps")
        s_h1 = sem("s_h1")
        s_h2ps = sem("s_h2ps")
        s_h2 = sem("s_h2")
        s_yps = sem("s_yps")
        s_ysb = sem("s_ysb")
        s_out = sem("s_out")
        s_pe_passed = sem("s_pe_passed")
        s_pool_passed = sem("s_pool_passed")

        w2_raw = pairs_flat[:, 0:NF * H]
        wt1_sb = pairs_flat[:, NF * H:NF * H + 3 * T1].rearrange("p (c n) -> p c n", c=3)
        wt1c_sb = pairs_flat[0:CTX, NF * H + 3 * T1:NF * H + 4 * T1]
        wt2_sb = emb_t_flat[:, 0:4 * T2].rearrange("p (c n) -> p c n", c=4)
        ctx_sb = ctx_all[0:CTX, :]
        w1_raw = outer_flat[:, 0:NF * H]
        w0a_raw = outer_flat[:, NF * H:NF * H + NCH * H]
        w0b_raw = outer_flat[:, NF * H + NCH * H:NF * H + 2 * NCH * H]
        w0s = outer_flat[:, NF * H + 2 * NCH * H:NF * H + 3 * NCH * H]
        w0_hi_f = w0_hi[:, :, :].rearrange("p c h -> p (c h)")
        w0_lo_f = w0_lo[:, :, :].rearrange("p c h -> p (c h)")
        b0_c, b2_c, b0x, b2x = (bias[:, i:i + 1] for i in range(4))
        N_PAIRS_ALL = NG * TG

        def chunk_rows(c):
            return min(P, NPAIR - c * P)

        def blocks_of(c):
            return 1 + sum(end < c * P + chunk_rows(c) for end in BLOCK_ENDS)

        def fields_of(k):
            return FIELDS4[k] * 4, min(4, NF - FIELDS4[k] * 4)

        def columns_of(k):
            f, m = fields_of(k)
            return slice(f * H, (f + m) * H)

        def unit_number(g, par, u):
            return u if g is None else count(g, sum(NU) // 2, NPU + par * (NU[0] - sum(NU) // 2) + u)

        def unit_bank(g, u):
            return y[u % YB] if g is None else scr[u % 2]

        def chunk_number(g, c):
            return c if g is None else count(g, NCH, NCH + c)

        def seq(g, par):
            return PRO_UNITS if g is None else UNITS[par]

        def prev_unit(g, par, u):
            if g is None:
                return (None, 0, u - YB) if u >= YB else None
            if u >= 2:
                return g, par, u - 2
            if isinstance(g, int) and g == 0:
                return None
            return g - 1, 1 - par, NU[1 - par] - 2 + u

        def pt_buffers(g, c):
            if g is None:
                return [(pt_hi[:, 0, :], pt_lo[:, 0, :]), (pt_hi[:, 1, :], pt_lo[:, 1, :]),
                        (x1_hi[:, 1, :], x1_lo[:, 1, :])][c % 3]
            return pt_hi[:, c % 2, :], pt_lo[:, c % 2, :]

        def chunks_before(units, u):
            return sum(e[0] == "T" for e in units[:u])

        w2_hi, w2_lo = w0_hi, w0_lo
        w2_hi_flat, w2_lo_flat = w0_hi_f, w0_lo_f
        o_hi = [w_hi[:, i * B:(i + 1) * B] for i in range(6)]
        o_lo = [w_lo[:, i * B:(i + 1) * B] for i in range(6)]
        x_sum0, x_sum2 = z0[:, :], scaled[:, 5, :]
        h1_ps = [scr[0], scr[1], y[0], y[1]]
        h2_ps = [y[2], y[3]]

        def tiles_of(ps):
            return ps[:, 0:TG * 2 * HALF1].rearrange("p (t q f) -> p t q f", t=TG, q=2)[:, :, :, 0:QF]

        block = es.enter_context(nc.Block())

        @block.sync
        def _(sp):
            sp.dma_start(ids_sb[:, :], ids).then_inc(s_ids, 16)
            sp.dma_start(first_sb[:, :], first_row).then_inc(s_ids, 16)
            sp.dma_start(ident[:, :], ident_in).then_inc(s_const, 16)
            sp.dma_start(bmask[:, :], bmask_in).then_inc(s_const, 16)
            sp.dma_start(bias[:, 0:1], b0).then_inc(s_const, 16)
            sp.dma_start(bias[:, 1:2], b2).then_inc(s_const, 16)
            sp.dma_start(bias[:, 4:8], bt1).then_inc(s_const, 16)
            sp.dma_start(bias[:, 8:10], bt2).then_inc(s_const, 16)
            sp.dma_start(bias[:, 10:12], wt3).then_inc(s_const, 16)
            sp.dma_start(sg[G_SLOTS.index(LAST4)][:, 3 * H:4 * H], b1.broadcast_to((P, H))).then_inc(s_const, 16)
            sp.dma_start(w0a_raw, w0a).then_inc(s_w0, 16)
            sp.dma_start(w0b_raw, w0b).then_inc(s_w0, 16)
            sp.dma_start(w1_raw, w1).then_inc(s_w1, 16)
            sp.wait_ge(s_pairs, N_PAIRS_ALL)
            sp.wait_ge(s_unit, unit_number(NG - 1, 1, 0))
            sp.dma_start(w2_raw, w2).then_inc(s_w2, 16)
            sp.dma_start(wt1_sb, wt1).then_inc(s_top, 16)
            sp.dma_start(wt1c_sb, wt1c).then_inc(s_top, 16)
            sp.dma_start(wt2_sb, wt2).then_inc(s_top, 16)
            sp.dma_start(ctx_sb, ctx_t).then_inc(s_top, 16)
            sp.wait_ge(s_ysb, 1)
            sp.dma_start(out, acc[0:1, 0:B]).then_inc(s_out, 16)
            sp.wait_ge(s_out, 16)

        @block.tensor
        def _(pe):
            def free_unit(g, par, u):
                before = prev_unit(g, par, u)
                if before is None:
                    return
                bg, bpar, bu = before
                units = seq(bg, bpar)
                if units[bu][0] == "T":
                    pe.wait_ge(s_lo, chunk_number(bg, chunks_before(units, bu)) + 1)
                else:
                    pe.wait_ge(s_unit_act, unit_number(bg, bpar, bu) + 1)

            def step_e(g, par, u, k, half, from_rows, rows_wait):
                free_unit(g, par, u)
                ps = unit_bank(g, u)
                if k == 0:
                    pe.wait_ge(*rows_wait)
                if k < 4:
                    for i in range(4):
                        last = nc.tensor.transpose(ps[0:QF, i * P:(i + 1) * P], from_rows[:, :, 4 * k + i],
                                                   ident[:, :])
                else:
                    if half == 0:
                        back = next(n for n in range(1, u + 1) if seq(g, par)[u - n] == ("E", 3))
                        pe.wait_ge(s_unit_act, unit_number(g, par, u - back) + 1)
                    if g is not None:
                        pe.sem_inc(s_pe_passed)
                    for t in range(TG):
                        b = half * GB + t * TB
                        last = nc.tensor.transpose(
                            ps[:, t * 2 * HALF1:t * 2 * HALF1 + HALF1 + QF],
                            emb_t[0:HALF1 + QF, b:b + TB, :].rearrange("p b d -> p (b d)"),
                            ident[0:HALF1 + QF, 0:HALF1 + QF])
                last.then_inc(s_unit, 1)

            def step_t(g, gpar, u, c, par, pairs_wait):
                free_unit(g, gpar, u)
                ps = unit_bank(g, u)
                if g is None:
                    pe.wait_ge(s_block, blocks_of(c))
                elif c == 0:
                    pe.wait_ge(s_pairs, pairs_wait)
                n = chunk_rows(c)
                for t in range(TG):
                    last = nc.tensor.transpose(ps[0:n, t * P:(t + 1) * P], pairs[:, par, t, c * P:c * P + n],
                                               ident[:, :])
                last.then_inc(s_unit, 1)

            def step_m(g, c, x1_free):
                pe.wait_ge(s_lo, chunk_number(g, c) + 1)
                if c == 0 and x1_free is not None:
                    pe.wait_ge(s_x1, x1_free)
                n = chunk_rows(c)
                hi, lo = pt_buffers(g, c)
                nc.tensor.matmul(ps_x1[:, :], w0_hi[0:n, c, :], hi[0:n, :], start=(c == 0), stop=False)
                nc.tensor.matmul(ps_x1[:, :], w0_lo[0:n, c, :], hi[0:n, :], start=False, stop=False)
                nc.tensor.matmul(ps_x1[:, :], w0_hi[0:n, c, :], lo[0:n, :], start=False,
                                 stop=(c == NCH - 1)).then_inc(s_l0, 1)

            def outer_products(g, t):
                n = count(g, TG, t)
                pe.wait_ge(s_chain, count(g, TG * CHAIN, (t + 1) * CHAIN))
                pe.wait_ge(s_embd, n + 1)
                if not (isinstance(n, int) and n == 0):
                    pe.wait_ge(s_outer_sb, n)
                nc.tensor.matmul(ps_g[:, 0:TB * NJ], x2[:, t % 2, :],
                                 embd[:, :, :].rearrange("p b j -> p (b j)"),
                                 start=True, stop=True).then_inc(s_outer, 1)

            def body(g, par, first=False, last=False):
                for s in range(NS):
                    t, k = divmod(s, NBK)
                    for what, i in PE_EXTRA[par].get(s, []):
                        u = UNITS[par].index((what, i)) if what != "M" else None
                        if last:
                            continue
                        if what == "T":
                            step_t(g, par, u, i, 1 - par, count(g, TG, TG))
                        elif what == "E":
                            step_e(g, par, u, i, par, rows[1 if first else 0],
                                   (s_rows[1], 16 * QF) if first else
                                   (s_rows[0], count(g, 16 * QF // PG, 16 * QF)))
                        else:
                            step_m(g, i, count(g, 2, 2))
                    if k == G_SLOT and (t or not first):
                        outer_products(g if t else g - 1, (t - 1) % TG)
                    if s == 0:
                        pe.wait_ge(s_x1, count(g, 2, 1))
                    if not (first and s < YB):
                        tb, kb = divmod((s - YB) % NS, NBK)
                        gb = g if s >= YB else g - 1
                        if KIND[kb] == "D":
                            pe.wait_ge(s_chain, count(gb, TG * CHAIN, tb * CHAIN + DONE[kb]))
                        else:
                            n = sum(KIND[i] != "D" for i in range(kb + 1))
                            pe.wait_ge(s_scaled, count(gb, TG * N_ACT, tb * N_ACT + n))
                    f, m = fields_of(k)
                    o = y[s % YB][:, 0:m * H]
                    if first and t == 0:
                        pe.wait_ge(s_w1lo, k + 1)
                    hi = x1_hi[:, par, t * P:(t + 1) * P]
                    lo = x1_lo[:, par, t * P:(t + 1) * P]
                    nc.tensor.matmul(o, hi, w_hi[:, f * H:(f + m) * H], start=True, stop=False)
                    nc.tensor.matmul(o, hi, w_lo[:, f * H:(f + m) * H], start=False, stop=False)
                    nc.tensor.matmul(o, lo, w_hi[:, f * H:(f + m) * H], start=False, stop=True).then_inc(s_y, 1)

            pe.wait_ge(s_const, 8 * 16)
            for u, (what, i, n) in enumerate(PRO):
                if what == "E":
                    step_e(None, 0, u, i, n, rows[0], (s_rows[0], 16 * QF))
                else:
                    if i == 0:
                        pe.wait_ge(s_w0lo, 1)
                    step_t(None, 0, u, i, 0, None)
                    if i >= 2:
                        step_m(None, i - 2, None)
            step_m(None, NCH - 2, None)
            step_m(None, NCH - 1, None)
            body(0, 0, first=True)
            with pe.Fori(0, NG // 2 - 1) as pair:
                body(pair * 2 + 1, 1)
                body(pair * 2 + 2, 0)
            body(NG - 1, 1, last=True)

            def h1_early(m):
                c = slice(m * P, (m + 1) * P)
                nc.tensor.matmul(h1_ps[m][:, :], wt1_sb[:, 0, c], x_sum0, start=True, stop=False)
                nc.tensor.matmul(h1_ps[m][:, :], wt1c_sb[:, c], ctx_sb, start=False, stop=False)

            pe.wait_ge(s_top, 4 * 16)
            pe.wait_ge(s_z, 1)
            pe.wait_ge(s_lo, NCH * NG)
            pe.wait_ge(s_unit_act, unit_number(NG - 1, 1, 0))
            h1_early(0)
            h1_early(1)
            outer_products(NG - 1, TG - 1)
            pe.wait_ge(s_scaled, NG * TG * N_ACT)
            h1_early(2)
            h1_early(3)
            pe.wait_ge(s_outer_sb, NG * TG)
            for m in range(4):
                nc.tensor.matmul(h1_ps[m][:, :], wt1_sb[:, 1, m * P:(m + 1) * P], outer[:, NF, :],
                                 start=False, stop=False)

            def fields3(j, half, start=False, stop=False):
                pe.wait_ge(s_w2lo, j + 3)
                for i in range(3):
                    pe.wait_ge(s_olo, j + (i + 1))
                    n = 3 * half + i
                    nc.tensor.matmul(ps_x1[:, :], w2_hi[:, n, :], o_hi[n], start=start and i == 0, stop=False)
                    nc.tensor.matmul(ps_x1[:, :], w2_lo[:, n, :], o_hi[n], start=False, stop=False)
                    nc.tensor.matmul(ps_x1[:, :], w2_hi[:, n, :], o_lo[n], start=False,
                                     stop=stop and i == 2).then_inc(s_l2, 1)

            fields3(0, 0, start=True)
            with pe.Fori(0, NF // 6 - 1) as six:
                fields3(six * 6 + 3, 1)
                fields3(six * 6 + 6, 0)
            fields3(NF - 6, 1)
            fields3(NF - 3, 0, stop=True)
            pe.wait_ge(s_z, 2)
            for m in range(4):
                nc.tensor.matmul(h1_ps[m][:, :], wt1_sb[:, 2, m * P:(m + 1) * P], x_sum2, start=False,
                                 stop=True).then_inc(s_h1ps, 1)
            for m in range(2):
                for c in range(4):
                    pe.wait_ge(s_h1, c + 1)
                    last = nc.tensor.matmul(h2_ps[m][:, :], wt2_sb[:, c, m * P:(m + 1) * P], scaled[:, c, :],
                                            start=(c == 0), stop=(c == 3))
                last.then_inc(s_h2ps, 1)
            for c in range(2):
                pe.wait_ge(s_h2, c + 1)
                last = nc.tensor.matmul(ps_g[0:1, :], bias[:, 10 + c:11 + c], scaled[:, 6 + c, :],
                                        start=(c == 0), stop=(c == 1))
            last.then_inc(s_yps, 1)

        @block.scalar
        def _(act):
            def unit(g, gpar, u, what, i, par):
                act.wait_ge(s_unit, unit_number(g, gpar, u) + 1)
                ps = unit_bank(g, u)
                if what == "T":
                    n = chunk_number(g, i)
                    if g is None:
                        if i >= 3:
                            act.wait_ge(s_l0, i - 2)
                    else:
                        act.wait_ge(s_l0, n - (1 if i >= 2 else i))
                    r = chunk_rows(i)
                    nc.scalar.copy(pt_buffers(g, i)[0][0:r, :], ps[0:r, :]).then_inc(s_unit_act, 1)
                elif i < 4:
                    if g is None and i == 0:
                        act.wait_ge(s_zero, 1)
                    for q in range(2):
                        last = nc.scalar.copy(
                            emb_t[q * HALF1:q * HALF1 + QF, :, 4 * i:4 * i + 4].rearrange("p b d -> p d b"),
                            ps[0:QF, :].rearrange("p (d q b) -> p q d b", d=4, q=2)[:, q])
                    last.then_inc(s_unit_act, 1)
                else:
                    if g is not None:
                        act.wait_ge(s_embs, count(g, 1, 1))
                    nc.scalar.copy(emb[:, par, :, :].rearrange("p t (q f) -> p t q f", q=2),
                                   tiles_of(ps)).then_inc(s_unit_act, 1)

            def x1_high(g, par, chunks, y_before):
                act.wait_ge(s_l0, chunks)
                if y_before is not None:
                    act.wait_ge(s_y, y_before)
                nc.scalar.activation(x1_hi[:, par, :], ps_x1[:, :], ACT.Identity, bias=b0_c,
                                     scale=1.0).then_inc(s_x1hi, 1)

            def outer_out(g, t):
                n = count(g, TG, t)
                act.wait_ge(s_outer, n + 1)
                nc.scalar.copy(outer[:, :, bass.ds(n * TB, TB)],
                               ps_g[:, 0:TB * NJ].rearrange("p (b j) -> p j b", b=TB)).then_inc(s_outer_sb, 1)

            def body(g, par, first=False, last=False):
                for s in range(NS):
                    t, k = divmod(s, NBK)
                    for what, i in ACT_EXTRA[par].get(s, []):
                        if not last:
                            unit(g, par, UNITS[par].index((what, i)), what, i, par)
                    if s == X1_ACT and not last:
                        x1_high(g, 1 - par, count(g, NCH, 2 * NCH), count(g, NS, 0) if not first else None)
                    if k == G_ACT and (t or not first):
                        outer_out(g if t else g - 1, (t - 1) % TG)
                    if KIND[k] == "D":
                        continue
                    if s == 0:
                        act.wait_ge(s_embs, count(g, 1, 1))
                    act.wait_ge(s_y, count(g, NS, s + 1))
                    f, m = fields_of(k)
                    fresh = first and t == 0
                    if KIND[k] == "V":
                        v = V_SLOTS.index(k)
                        dst = sv[v]
                        if not fresh:
                            after = DONE[D_SLOTS[0]] if v == 0 else DONE["V"]
                            act.wait_ge(s_chain, count(g, TG * CHAIN, (t - 1) * CHAIN + after))
                    else:
                        v = G_SLOTS.index(k)
                        dst = sg[v]
                        if not fresh:
                            act.wait_ge(s_gadd, count(g, TG * 2, (t - 1) * 2 + (1 if v < 2 else 2)))
                    for i in range(m):
                        last_i = nc.scalar.mul(dst[:, i * H:(i + 1) * H], y[s % YB][:, i * H:(i + 1) * H],
                                               embs[:, par, t, f + i:f + i + 1])
                    last_i.then_inc(s_scaled, 1)

            act.wait_ge(s_const, 8 * 16)
            nc.scalar.mul(bias[:, 2:4], bias[:, 0:2], float(D))
            act.wait_ge(s_w0sum, 1)
            nc.scalar.copy(w0_hi_f, w0s).then_inc(s_w0hi, 1)

            def weights_high(n):
                act.wait_ge(s_w1, 16)
                c = columns_of(n)
                nc.scalar.copy(w_hi[:, c], w1_raw[:, c]).then_inc(s_w1hi, 1)

            for n in range(NBK):
                weights_high(n)
            for u, (what, i, n) in enumerate(PRO):
                unit(None, 0, u, what, i, n)
            x1_high(None, 0, NCH, None)
            body(0, 0, first=True)
            with act.Fori(0, NG // 2 - 1) as pair:
                body(pair * 2 + 1, 1)
                body(pair * 2 + 2, 0)
            act.wait_ge(s_x1, 2 * NG)
            nc.scalar.activation(x_sum0, z0[:, :], ACT.Identity, bias=b0x, scale=1.0).then_inc(s_z, 1)
            body(NG - 1, 1, last=True)
            outer_out(NG - 1, TG - 1)

            def high3(j, half, free=None):
                c = slice(3 * half * H, 3 * (half + 1) * H)
                if free is not None:
                    act.wait_ge(s_l2, free)
                nc.scalar.copy(w2_hi_flat[:, c], w2_raw[:, bass.ds(j * H, 3 * H)]).then_inc(s_w2hi, 1)
                for i in range(3):
                    nc.scalar.copy(o_hi[3 * half + i],
                                   outer_flat[:, bass.ds((j + i) * B, B)]).then_inc(s_ohi, 1)

            act.wait_ge(s_w2, 16)
            act.wait_ge(s_l0, NCH * NG)
            act.wait_ge(s_outer_sb, NG * TG)
            act.wait_ge(s_y, NS * NG)
            high3(0, 0)
            high3(3, 1)
            with act.Fori(1, NF // 6) as six:
                high3(six * 6, 0, six * 6 - 3)
                high3(six * 6 + 3, 1, six * 6)
            high3(NF - 3, 0, NF - 6)
            act.wait_ge(s_l2, NF)
            nc.scalar.activation(x_sum2, ps_x1[:, :], ACT.Identity, bias=b2x, scale=1.0).then_inc(s_z, 1)
            for m in range(4):
                act.wait_ge(s_h1ps, m + 1)
                nc.scalar.activation(scaled[:, m, :], h1_ps[m][:, :], ACT.Relu, bias=bias[:, 4 + m:5 + m],
                                     scale=1.0).then_inc(s_h1, 1)
            for m in range(2):
                act.wait_ge(s_h2ps, m + 1)
                nc.scalar.activation(scaled[:, 6 + m, :], h2_ps[m][:, :], ACT.Relu, bias=bias[:, 8 + m:9 + m],
                                     scale=1.0).then_inc(s_h2, 1)
            act.wait_ge(s_yps, 1)
            nc.scalar.copy(acc[0:1, 0:B], ps_g[0:1, :]).then_inc(s_ysb, 1)

        def tile_pairs(eng, par, t, blocks=range(len(FBLOCKS))):
            for i in blocks:
                (a, m), at = FBLOCKS[i], BLOCK_ENDS[i] - BLOCK_PAIRS[i]
                n = NF - a
                last = eng.tensor_tensor(
                    pairs[:, par, t, at:at + m * n].rearrange("p (j k) -> p j k", j=m),
                    emb[:, par, t, a:a + m].unsqueeze(2).broadcast_to((P, m, n)),
                    emb[:, par, t, a:NF].unsqueeze(1).broadcast_to((P, m, n)), ALU.mult)
            return last

        @block.vector
        def _(dve):
            def chunk_low(g, par, c, u):
                dve.wait_ge(s_unit_act, unit_number(g, par, u) + 1)
                r = chunk_rows(c)
                hi, lo = pt_buffers(g, c)
                nc.vector.tensor_tensor(lo[0:r, :], unit_bank(g, u)[0:r, :], hi[0:r, :].bitcast(F32),
                                        ALU.subtract).then_inc(s_lo, 1)

            def x1_low(g1, par):
                dve.wait_ge(s_x1hi, count(g1, 1, 1))
                nc.vector.scalar_tensor_tensor(out=x1_lo[:, par, :], in0=ps_x1[:, :], scalar=b0_c,
                                               in1=x1_hi[:, par, :].bitcast(F32), op0=ALU.add,
                                               op1=ALU.subtract).then_inc(s_x1, 1)
                nc.vector.reduce_sum(z0[:, bass.ds(g1 * GB, GB)],
                                     ps_x1[:, :].rearrange("p (b d) -> p b d", d=D),
                                     axis=AX.X).then_inc(s_x1, 1)

            def body(g, par, first=False, last=False):
                for s in range(NS):
                    t, k = divmod(s, NBK)
                    base = t * CHAIN

                    def chained(n):
                        v = count(g, TG * CHAIN, base + n)
                        if not (isinstance(v, int) and v <= 0):
                            dve.wait_ge(s_chain, v)

                    for what, i in DVE_EXTRA[par].get(s, []):
                        if not last:
                            chunk_low(g, par, i, UNITS[par].index((what, i)))
                    if s == X1_DVE and not last:
                        x1_low(g + 1, 1 - par)
                    if s == 0:
                        dve.wait_ge(s_embs, count(g, 1, 1))
                    for step in [w for w, at in STEPS if at == k]:
                        if step in D_SLOTS:
                            f, m = fields_of(step)
                            bank = y[(t * NBK + step) % YB]
                            dve.wait_ge(s_y, count(g, NS, t * NBK + step + 1))
                            start = step == D_SLOTS[0]
                            if start:
                                a = sum(KIND[i] != "D" for i in range(V_SLOTS[0] + 1))
                                dve.wait_ge(s_scaled, count(g, TG * N_ACT, t * N_ACT + a))
                            for i in range(m):
                                b = slice(i * H, (i + 1) * H)
                                if start and i == 0:
                                    chained(DONE["F"] - CHAIN)
                                elif not start:
                                    chained(DONE[D_SLOTS[D_SLOTS.index(step) - 1]] - 4 + i + 1)
                                nc.vector.scalar_tensor_tensor(
                                    out=acc[:, b], in0=bank[:, b], scalar=embs[:, par, t, f + i:f + i + 1],
                                    in1=sv[0][:, b] if start else acc[:, b],
                                    op0=ALU.mult, op1=ALU.add).then_inc(s_chain, 1)
                        elif step == "V":
                            a = sum(KIND[i] != "D" for i in range(V_SLOTS[2] + 1))
                            dve.wait_ge(s_scaled, count(g, TG * N_ACT, t * N_ACT + a))
                            chained(0)
                            nc.vector.tensor_tensor(acc_b[:, :], sv[1], sv[2], ALU.add).then_inc(s_chain, 1)
                        elif step == "G":
                            dve.wait_ge(s_gadd, count(g, TG * 2, t * 2 + 2))
                            chained(DONE["V"])
                            nc.vector.tensor_tensor(acc_b[:, :], acc_b[:, :], gsum[1],
                                                    ALU.add).then_inc(s_chain, 1)
                        elif step == "A":
                            chained(DONE["G"])
                            nc.vector.tensor_tensor(acc[:, :], acc[:, :], acc_b[:, :],
                                                    ALU.add).then_inc(s_chain, 1)
                        elif step == "F":
                            chained(DONE["A"])
                            nc.vector.tensor_tensor(acc_b[:, 0:256], acc[:, 0:256], acc[:, 256:512],
                                                    ALU.add).then_inc(s_chain, 1)
                        else:
                            chained(DONE["F"])
                            tile_before = count(g, TG, t - 1)
                            if not (isinstance(tile_before, int) and tile_before <= 0):
                                dve.wait_ge(s_outer, tile_before)
                            nc.vector.tensor_tensor(x2[:, t % 2, :], acc_b[:, 0:H], acc_b[:, H:2 * H],
                                                    ALU.add).then_inc(s_chain, 1)

            nc.vector.memset(emb_t[:, :, :], 0.0).then_inc(s_zero, 1)
            dve.wait_ge(s_w0, 32)
            nc.vector.tensor_tensor(w0s, w0a_raw, w0b_raw, ALU.add).then_inc(s_w0sum, 1)
            dve.wait_ge(s_w0hi, 1)
            nc.vector.tensor_tensor(w0_lo_f, w0s, w0_hi_f.bitcast(F32), ALU.subtract).then_inc(s_w0lo, 1)

            def weights_low(n):
                dve.wait_ge(s_w1hi, n + 1)
                c = columns_of(n)
                nc.vector.tensor_tensor(w_lo[:, c], w1_raw[:, c], w_hi[:, c].bitcast(F32),
                                        ALU.subtract).then_inc(s_w1lo, 1)

            for n in range(NBK):
                weights_low(n)
            dve.wait_ge(s_unit_act, PRO.index(("E", 4, 0)) + 1)
            c = 0
            for i in range(len(FBLOCKS)):
                while c < NCH and blocks_of(c) < i:
                    chunk_low(None, 0, c, PRO.index(("T", c, 0)))
                    c += 1
                for t in range(TG):
                    last = tile_pairs(nc.vector, 0, t, [i])
                last.then_inc(s_block, 1)
            for c in range(c, NCH):
                chunk_low(None, 0, c, PRO.index(("T", c, 0)))
            x1_low(0, 0)
            dve.wait_ge(s_unit_act, PRO.index(("E", 4, 1)) + 1)
            for t in range(TG):
                tile_pairs(nc.vector, 1, t).then_inc(s_pairs, 1)
            body(0, 0, first=True)
            with dve.Fori(0, NG // 2 - 1) as pair:
                body(pair * 2 + 1, 1)
                body(pair * 2 + 2, 0)
            body(NG - 1, 1, last=True)
            def low3(j, half):
                for i in range(3):
                    dve.wait_ge(s_ohi, j + (i + 1))
                    nc.vector.tensor_tensor(o_lo[3 * half + i], outer_flat[:, bass.ds((j + i) * B, B)],
                                            o_hi[3 * half + i].bitcast(F32), ALU.subtract).then_inc(s_olo, 1)

            low3(0, 0)
            with dve.Fori(0, NF // 6) as six:
                low3(six * 6 + 3, 1)
                low3(six * 6 + 6, 0)

        @block.gpsimd
        def _(pool):
            def row_numbers(at, buffer):
                pool.sem_inc(s_pool_passed)
                nc.gpsimd.tensor_tensor(idx[:, buffer, :], ids_sb[:, bass.ds(at, QF)], first_sb[:, :],
                                        ALU.add).then_inc(s_idx, 2)

            def gather(buffer, i):
                nc.gpsimd.indirect_dma_start(
                    out=rows[buffer][:, i, :], out_offset=None, in_=table,
                    in_offset=bass.IndirectOffsetOnAxis(ap=idx[:, buffer, i:i + 1], axis=0)).then_inc(s_rows[buffer], 16)

            def copy_embs(par):
                pool.sem_inc(s_pool_passed)
                nc.gpsimd.tensor_copy(embs[:, par, :, 0:NF], emb[:, par, :, 0:NF]).then_inc(s_embs, 1)

            def block_diagonal(g, par, t):
                n = count(g, TG, t)
                if not (isinstance(n, int) and n < 1):
                    pool.wait_ge(s_outer, n)
                nc.gpsimd.tensor_tensor(embd[:, :, :],
                                        embs[:, par, t, :].unsqueeze(1).broadcast_to((P, TB, NJ)),
                                        bmask[:, :].unsqueeze(2).broadcast_to((P, TB, NJ)),
                                        ALU.mult).then_inc(s_embd, 1)

            def add(g, t, which, first):
                slot = G_SLOTS[which + 1]
                a = sum(KIND[i] != "D" for i in range(slot + 1))
                pool.wait_ge(s_scaled, count(g, TG * N_ACT, t * N_ACT + a))
                if which == 0:
                    if not (first and t == 0):
                        pool.wait_ge(s_gadd, count(g, TG * 2, t * 2))
                    nc.gpsimd.tensor_tensor(gsum[0], sg[0], sg[1], ALU.add).then_inc(s_gadd, 1)
                else:
                    pool.wait_ge(s_gadd, count(g, TG * 2, t * 2 + 1))
                    if not (first and t == 0):
                        pool.wait_ge(s_chain, count(g, TG * CHAIN, (t - 1) * CHAIN + DONE["G"]))
                    nc.gpsimd.tensor_tensor(gsum[1], gsum[0], sg[2], ALU.add).then_inc(s_gadd, 1)

            def body(g, par, first=False, last=False):
                pool.wait_ge(s_embs, count(g, 1, 1))
                pool.sem_inc(s_pool_passed)
                for (what, i), _ in sorted(POOL_AT[par].items(), key=lambda x: x[1]):
                    if what == "diagonal":
                        block_diagonal(g, par, i)
                    elif what == "add":
                        add(g, i // 2, i % 2, first)
                    elif last:
                        continue
                    elif what == "copy":
                        if first:
                            pool.wait_ge(s_unit_act, PRO.index(("E", 4, 1)) + 1)
                        else:
                            pool.wait_ge(s_embd, count(g, TG, 0))
                            pool.wait_ge(s_scaled, count(g, TG * N_ACT, 0))
                            pool.wait_ge(s_chain, count(g, TG * CHAIN, DONE["A"] - CHAIN))
                        copy_embs(1 - par)
                    elif what == "gather":
                        if i == 0:
                            if not first:
                                pool.wait_ge(s_unit, unit_number(g, par, UNITS[par].index(("E", 3))) + 1)
                            row_numbers(count(g, QF // PG, 2 * QF), 0)
                            pool.wait_ge(s_idx, count(g, 1, 6))
                            pool.sem_inc(s_pool_passed)
                        gather(0, i)
                    else:
                        if i == 0:
                            pool.wait_ge(s_unit_act, unit_number(g, par, UNITS[par].index(("E", 4))) + 1)
                            pool.wait_ge(s_unit, NPU if first else
                                         unit_number(g - 1, 1 - par, UNITS[1 - par].index(("T", NCH - 1))) + 1)
                        tile_pairs(nc.gpsimd, par, i).then_inc(s_pairs, 1)

            nc.gpsimd.memset(embs[:, :, :, NF:NJ], 1.0).then_inc(s_ones, 1)
            pool.wait_ge(s_ids, 32)
            for buffer in range(2):
                row_numbers(buffer * QF, buffer)
                pool.wait_ge(s_idx, 2 * (buffer + 1))
                for i in range(QF):
                    gather(buffer, i)
                    if (buffer, i) == (1, COPY0_AT):
                        pool.wait_ge(s_ones, 1)
                        pool.wait_ge(s_const, 8 * 16)
                        pool.wait_ge(s_unit_act, PRO.index(("E", 4, 0)) + 1)
                        copy_embs(0)
            body(0, 0, first=True)
            with pool.Fori(0, NG // 2 - 1) as pair:
                body(pair * 2 + 1, 1)
                body(pair * 2 + 2, 0)
            body(NG - 1, 1, last=True)
            pool.wait_ge(s_rows[0], 16 * QF * (NIDX // PG - 1) - 16 * (QF - N_EVEN))
            def weights3(j, half, threes):
                c = slice(3 * half * H, 3 * (half + 1) * H)
                pool.wait_ge(s_w2hi, threes)
                pool.sem_inc(s_pool_passed)
                nc.gpsimd.tensor_tensor(w2_lo_flat[:, c], w2_raw[:, bass.ds(j * H, 3 * H)],
                                        w2_hi_flat[:, c].bitcast(F32), ALU.subtract).then_inc(s_w2lo, 3)

            weights3(0, 0, 1)
            with pool.Fori(0, NF // 6) as six:
                weights3(six * 6 + 3, 1, six * 2 + 2)
                weights3(six * 6 + 6, 0, six * 2 + 3)


def _layout(inputs):
    a = {k: np.asarray(v) for k, v in inputs.items()}
    table = np.concatenate([a[f"tbl_{f}"] for f in range(NF)], axis=0)
    ids = np.zeros((NIDX * GB, NJ), a["ids"].dtype)
    ids[0:B, 0:NF] = a["ids"]
    ids = ids.reshape(NIDX // PG, GB2, 2, QF).transpose(2, 1, 0, 3).reshape(P, NIDX // PG * QF)
    first = np.zeros(NJ, np.int32)
    first[0:NF] = np.cumsum([0] + VOCAB[:-1])
    first_row = np.repeat(first.reshape(2, 1, QF), GB2, axis=1).reshape(P, QF)
    ident = np.eye(P, dtype=np.float32)
    bmask = np.repeat(np.eye(TB, dtype=np.float32), D, axis=0)
    w0 = a["L0_rec_W0"].reshape(H, NF, NF)
    w0a = np.zeros((NCH * P, H), w0.dtype)
    w0b = np.zeros((NCH * P, H), w0.dtype)
    at = 0
    for f, m in FBLOCKS:
        n = NF - f
        w0a[at:at + m * n] = w0[:, f:f + m, f:].reshape(H, m * n).T
        other = w0[:, f:, f:f + m].transpose(2, 1, 0).copy()
        other[:, 0:m] = 0
        w0b[at:at + m * n] = other.reshape(m * n, H)
        at += m * n

    def chunks(x, n):
        return x.reshape(n, P, -1).transpose(1, 0, 2)

    def by_field(w):
        return w.reshape(H, NF, H).transpose(2, 1, 0).reshape(H, NF * H)

    return [
        ("table", table), ("ids_g", ids), ("first_row", first_row), ("ident_c", ident), ("bmask_c", bmask),
        ("w0a", chunks(w0a, NCH).reshape(P, NCH * H)), ("w0b", chunks(w0b, NCH).reshape(P, NCH * H)),
        ("w1", by_field(a["L0_rec_W1"])), ("w2", by_field(a["L0_rec_W2"])),
        ("b0", a["L0_rec_b0"].reshape(P, 1)), ("b1", a["L0_rec_b1"].reshape(1, H)),
        ("b2", a["L0_rec_b2"].reshape(P, 1)),
        ("wt1", chunks(a["W_top1"][0:3 * H], 3)), ("wt1c", a["W_top1"][3 * H:]),
        ("bt1", a["b_top1"].reshape(4, P).T), ("wt2", chunks(a["W_top2"], 4)),
        ("bt2", a["b_top2"].reshape(2, P).T), ("wt3", a["W_top3"].reshape(2, P).T),
        ("ctx_t", a["dense_ctx"].T),
    ]


def kernel(**inputs):
    import concourse.bacc as bacc
    from concourse.bass_utils import run_bass_kernel_spmd

    nc = bacc.Bacc("TRN2", target_bir_lowering=False, num_devices=1)
    arrays, args = {}, []
    for name, a in _layout(inputs):
        a = np.ascontiguousarray(a)
        arrays[f"in_{name}"] = a
        args.append(nc.dram_tensor(f"in_{name}", a.shape, mybir.dt.from_np(a.dtype), kind="ExternalInput").ap())
    res = nc.dram_tensor("out_0", (1, B), F32, kind="ExternalOutput").ap()
    build(nc, *args, res)
    r = run_bass_kernel_spmd(nc, [arrays], core_ids=[0])
    return r.results[0]["out_0"].reshape(B, 1)
```
